# Optimizing a Trainium2 kernel written in Bass

```python
import numpy as np
import jax
import jax.numpy as jnp

def _softmax(x, axis=-1):
    return jax.nn.softmax(x, axis=axis)

def _gelu(x):
    return jax.nn.gelu(x, approximate=True)

def _silu(x):
    return jax.nn.silu(x)

def _sigmoid(x):
    return jax.nn.sigmoid(x)

def _layernorm(x, axis=-1, eps=1e-05):
    m = jnp.mean(x, axis=axis, keepdims=True)
    v = jnp.var(x, axis=axis, keepdims=True)
    return (x - m) / jnp.sqrt(v + eps)

def _scatter_add(tgt, idx, src, axis=0):
    return tgt.at[idx].add(src)

def _segment_sum(src, seg, n):
    return jax.ops.segment_sum(src, seg, n)
kernel_name = 'mk_conv_preact_d2_conv_nhwc512_r2_5e03ec'

def setup_inputs(seed: int=0):
    np.random.seed(seed)
    _w = jnp.asarray

    def _rec_inputs():
        import jax
        import jax.numpy as jnp
        _gk = jax.random.key(seed)
        x = -0.0003929 + 0.9999 * jax.random.normal(jax.random.fold_in(_gk, 1), (8, 32, 32, 256), jnp.float32)
        return x
    x = _rec_inputs()

    def _L0_conv_setup():
        import jax, jax.numpy as jnp
        import numpy as np
        DIM = 256
        NUM_HEADS = 8
        B, NW, W = (8, 32, 32)
        key = jax.random.key(seed)
        k1, k2, k3 = jax.random.split(key, 3)
        x = jax.random.normal(k1, (B, NW, W, DIM), dtype=jnp.float32)
        w_qkv = jax.random.normal(k2, (DIM, 3 * DIM), dtype=jnp.float32) * DIM ** (-0.5)
        w_proj = jax.random.normal(k3, (DIM, DIM), dtype=jnp.float32) * DIM ** (-0.5)
        b_proj = jnp.zeros((DIM,), dtype=jnp.float32)
        return {'x': x, 'w_qkv': w_qkv, 'w_proj': w_proj, 'b_proj': b_proj}
    _L0_conv_all = _L0_conv_setup()
    _L0_conv_in = {k: v for k, v in _L0_conv_all.items() if k in ('w_qkv', 'w_proj', 'b_proj')}
    del _L0_conv_all

    def _L1_conv_setup():
        import jax, jax.numpy as jnp
        import numpy as np
        key = jax.random.key(seed)
        k1, k2, k3, k4, k5 = jax.random.split(key, 5)
        B, H, W, C = (4, 32, 32, 256)
        ratio = 8
        d = C // ratio
        x = jax.random.normal(k1, (B, H, W, C), dtype=jnp.float32)
        Wq = jax.random.normal(k2, (C, d), dtype=jnp.float32) * np.sqrt(2.0 / C)
        Wk = jax.random.normal(k3, (C, d), dtype=jnp.float32) * np.sqrt(2.0 / C)
        Wv = jax.random.normal(k4, (C, C), dtype=jnp.float32) * np.sqrt(2.0 / C)
        gamma = jax.random.normal(k5, (1,), dtype=jnp.float32)
        return {'x': x, 'Wq': Wq, 'Wk': Wk, 'Wv': Wv, 'gamma': gamma}
    _L1_conv_all = _L1_conv_setup()
    _L1_conv_in = {k: v for k, v in _L1_conv_all.items() if k in ('Wq', 'Wk', 'Wv', 'gamma')}
    del _L1_conv_all
    return {'x': x, 'L0_conv_w_qkv': _L0_conv_in['w_qkv'], 'L0_conv_w_proj': _L0_conv_in['w_proj'], 'L0_conv_b_proj': _L0_conv_in['b_proj'], 'L1_conv_Wq': _L1_conv_in['Wq'], 'L1_conv_Wk': _L1_conv_in['Wk'], 'L1_conv_Wv': _L1_conv_in['Wv'], 'L1_conv_gamma': _L1_conv_in['gamma']}

def reference(x, L0_conv_w_qkv, L0_conv_w_proj, L0_conv_b_proj, L1_conv_Wq, L1_conv_Wk, L1_conv_Wv, L1_conv_gamma):
    import jax
    import jax.numpy as jnp

    def _L0_conv_ref(x, w_qkv, w_proj, b_proj):
        import jax, jax.numpy as jnp
        import numpy as np
        DIM = 256
        NUM_HEADS = 8
        B, NW, W = (8, 32, 32)
        batch, nw, w, dim = x.shape
        heads = NUM_HEADS
        dh = dim // heads
        scale = dh ** (-0.5)
        qkv = jnp.einsum('bnwc,cd->bnwd', x, w_qkv)
        qkv = qkv.reshape(batch, nw, w, 3, heads, dh)
        qkv = jnp.transpose(qkv, (3, 0, 4, 1, 2, 5))
        q, k, v = (qkv[0], qkv[1], qkv[2])
        attn = jnp.einsum('bhnqd,bhnkd->bhnqk', q, k) * scale
        attn = jax.nn.softmax(attn, axis=-1)
        out = jnp.einsum('bhnqk,bhnkd->bhnqd', attn, v)
        out = out.reshape(batch, nw, w, dim)
        return jnp.einsum('bnwc,cd->bnwd', out, w_proj) + b_proj

    def _L1_conv_ref(x, Wq, Wk, Wv, gamma):
        import jax, jax.numpy as jnp
        import numpy as np
        B, H, W, C = x.shape
        N = H * W
        q = jnp.einsum('bhwc,cd->bhwd', x, Wq).reshape(B, N, -1)
        k = jnp.einsum('bhwc,cd->bhwd', x, Wk).reshape(B, N, -1)
        v = jnp.einsum('bhwc,cd->bhwd', x, Wv).reshape(B, N, C)
        energy = jnp.einsum('bid,bjd->bij', k, q)
        attn = jax.nn.softmax(energy, axis=-1)
        out = jnp.einsum('bij,bjc->bic', attn, v)
        out = out.reshape(B, H, W, C)
        return gamma * out

    def _gn(v, G=32, eps=1e-05):
        B_, H_, W_, C_ = v.shape
        g = v.reshape(B_, H_, W_, G, C_ // G)
        m = jnp.mean(g, axis=(1, 2, 4), keepdims=True)
        s = jnp.var(g, axis=(1, 2, 4), keepdims=True)
        return ((g - m) / jnp.sqrt(s + eps)).reshape(v.shape)

    def _ln_c(v, eps=1e-06):
        m = jnp.mean(v, axis=-1, keepdims=True)
        s = jnp.var(v, axis=-1, keepdims=True)
        return (v - m) / jnp.sqrt(s + eps)

    def _ln_t(v, eps=1e-05):
        m = jnp.mean(v, axis=-1, keepdims=True)
        s = jnp.var(v, axis=-1, keepdims=True)
        return (v - m) / jnp.sqrt(s + eps)

    def _to_tokens(v):
        B_, H_, W_, C_ = v.shape
        return v.reshape(B_, H_ * W_, C_)

    def _from_tokens(t, like):
        return t.reshape(like.shape)
    x = x + _L0_conv_ref(_gn(x), L0_conv_w_qkv, L0_conv_w_proj, L0_conv_b_proj)
    x = x + _L1_conv_ref(_gn(x), L1_conv_Wq, L1_conv_Wk, L1_conv_Wv, L1_conv_gamma)
    return x

_drawn_inputs = setup_inputs


def setup_inputs(seed=0):
    import zlib

    import numpy as np

    out = dict(_drawn_inputs(seed))
    spreads = {'L0_conv_b_proj': (0.0, 0.1)}
    factors = {}
    for name, (base, spread) in spreads.items():
        noise = np.random.default_rng([zlib.crc32(name.encode()), seed]).standard_normal(out[name].shape)
        drawn = base * np.exp(spread * noise) if base else spread * noise
        out[name] = jnp.asarray(drawn.astype(out[name].dtype))
    for name, factor in factors.items():
        out[name] = (out[name] * factor).astype(out[name].dtype)
    return out
```

```python
import concourse.bass as bass
from concourse import mybir
from contextlib import ExitStack

F32 = mybir.dt.float32
F16 = mybir.dt.float16
ALU = mybir.AluOpType
ACT = mybir.ActivationFunctionType
X = mybir.AxisListType.X

P = 128
IMAGES, TOKENS, CH = 8, 1024, 256
TILES = TOKENS // P
CT = CH // P
CHUNK = 512
CHUNKS = TOKENS // CHUNK
TPC = CHUNK // P
HEADS, DH = 8, 32
WIN = 32
GROUP = 8
VCOL = CH + 2
EPS = 1e-5
ROW_SCALE = 2.0 ** 15


def nth(b, per, n):
    return b * per + n


def build(nc, x, w_qkv, w_proj, b_proj, wq1, wk1, wv1, gamma, ident_d, group_d, masks_d, out):
    x_v = x.rearrange("b (t y) w c -> b t (y w) c", t=TILES)
    out_v = out.rearrange("b (t y) w c -> b t (y w) c", t=TILES)

    with ExitStack() as ctx:
        def sb(name, shape, dt=F32):
            return ctx.enter_context(nc.sbuf_tensor(name, shape, dt))

        def sem(name):
            return ctx.enter_context(nc.semaphore(name))

        ident = sb("ident", [P, P])
        group_avg = sb("group_avg", [P, P])
        masks = sb("masks", [P, 2])
        bias = sb("bias", [P, CH])
        gam = sb("gam", [P, 1])
        wqkv_h, wqkv_l = sb("wqkv_h", [P, CT, 3 * CH], F16), sb("wqkv_l", [P, CT, 3 * CH], F16)
        wp_h, wp_l = sb("wp_h", [P, CT, CH], F16), sb("wp_l", [P, CT, CH], F16)
        wqk1_h, wqk1_l = sb("wqk1_h", [P, CT, P], F16), sb("wqk1_l", [P, CT, P], F16)
        wv1_h, wv1_l = sb("wv1_h", [P, CT, CH], F16), sb("wv1_l", [P, CT, CH], F16)
        wmax = sb("wmax", [P, 5])
        wmax_all = sb("wmax_all", [5, 1])
        wmax_diag = sb("wmax_diag", [5, 5])
        ones5 = sb("ones5", [5, P])
        unit = sb("unit", [P, 5])
        unit_inv = sb("unit_inv", [P, 5])
        f_q = sb("f_q", [P, 1])
        f_proj = sb("f_proj", [P, 1])
        f_energy = sb("f_energy", [P, 1])
        f_out = sb("f_out", [P, 1])
        minus_half = sb("minus_half", [P, CT])
        xin = sb("xin", [P, TILES, CH])
        xb = sb("xb", [P, TILES, CH])
        x1 = sb("x1", [P, TILES, CH])
        a_xT = sb("a_xT", [P, CT, TOKENS])
        xn32 = [sb(f"xn32_{n}", [P, CHUNKS * CT, CHUNK]) for n in range(1)]
        a_nh, a_nl = sb("a_nh", [P, CT, TOKENS], F16), sb("a_nl", [P, CT, TOKENS], F16)
        qkT = sb("qkT", [P, 4, TOKENS])
        v_tok = sb("v_tok", [P, TILES, CH])
        s32 = sb("s32", [P, CHUNKS, TPC * CH])
        pT = sb("pT", [P, CHUNKS, TPC * CH])
        o_src = sb("o_src", [P, 4, 2, 2, 2, P], F16)
        o_dst = sb("o_dst", [P, 4, 2, 2, 2, P], F16)
        a_rmax, a_rsum = sb("a_rmax", [P, CHUNKS, 32]), sb("a_rsum", [P, CHUNKS, 32])
        a_rinv = sb("a_rinv", [P, CHUNKS, 32])
        y = sb("y", [P, TILES, CH])
        b_xT = a_xT
        b_nh, b_nl = sb("b_nh", [P, CT, TOKENS], F16), sb("b_nl", [P, CT, TOKENS], F16)
        b_xTs = sb("b_xTs", [P, CT, TOKENS])
        qk_h = sb("qk_h", [P, TOKENS], F16)
        qk_hl = sb("qk_hl", [P, TOKENS], F16)
        q_stack = sb("q_stack", [P, TOKENS], F16)
        k_stack = sb("k_stack", [P, TOKENS], F16)
        v_h, v_l = sb("v_h", [P, TILES, VCOL], F16), sb("v_l", [P, TILES, VCOL], F16)
        max_neg = sb("max_neg", [P, TILES])
        max_dup = sb("max_dup", [P, TILES, 2])
        max_row = sb("max_row", [P, TOKENS], F16)
        e32 = sb("e32", [P, 2, TOKENS])
        e_h, e_l = sb("e_h", [P, TILES, TOKENS], F16), sb("e_l", [P, TILES, TOKENS], F16)
        y_inv = sb("y_inv", [P, TILES])
        y_fac = sb("y_fac", [P, TILES])
        norm = {k: dict(st=sb(k + "st", [P, CT, CHUNKS, 6]), mv=sb(k + "mv", [P, CT, 2]),
                        gm=sb(k + "gm", [P, CT]), d=sb(k + "d", [P, CT]), e=sb(k + "e", [P, CT]),
                        ve=sb(k + "ve", [P, CT]), r=sb(k + "r", [P, CT]), nb=sb(k + "nb", [P, CT])) for k in "ab"}
        stage = e_l[:].rearrange("p t n -> p (t n)").bitcast(F32)
        wqkv_f = stage[:, 0:1536].rearrange("p (a n) -> p a n", a=CT)
        wp_f = stage[:, 1536:2048].rearrange("p (a n) -> p a n", a=CT)
        wqk1_f = stage[:, 2048:2304].rearrange("p (a n) -> p a n", a=CT)
        wv1_f = stage[:, 2304:2816].rearrange("p (a n) -> p a n", a=CT)
        weights = [(wqkv_f, wqkv_h, wqkv_l), (wp_f, wp_h, wp_l), (wqk1_f, wqk1_h, wqk1_l), (wv1_f, wv1_h, wv1_l)]

        pa = ctx.enter_context(nc.psum_tensor("pa", [P, 4, CHUNK], F32))
        pb = ctx.enter_context(nc.psum_tensor("pb", [P, 4, CHUNK], F32))

        s_const, s_w, s_chain = sem("s_const"), sem("s_w"), sem("s_chain")
        s_wmax, s_wmaxT, s_diag, s_unit_ps, s_ready = sem("s_wmax"), sem("s_wmaxT"), sem("s_diag"), sem("s_unit_ps"), sem("s_ready")
        s_pool = sem("s_pool")
        a_load = [sem(f"a_load{c}") for c in range(CHUNKS)]
        a_xb = sem("a_xb")
        a_x1 = sem("a_x1")
        a_s = sem("a_s")
        a_o = sem("a_o")
        a_y = sem("a_y")
        a_qk = sem("a_qk")
        a_v = sem("a_v")
        a_qke = sem("a_qke")
        a_ve = sem("a_ve")
        a_max = sem("a_max")
        a_sub = sem("a_sub")
        a_exp = sem("a_exp")
        a_sum = sem("a_sum")
        a_inv = sem("a_inv")
        a_prob = sem("a_prob")
        a_pt = sem("a_pt")
        a_oh = sem("a_oh")
        a_ol = sem("a_ol")
        a_ox = sem("a_ox")
        b_copy = sem("b_copy")
        b_qk = sem("b_qk")
        b_qkh = sem("b_qkh")
        b_qkl = sem("b_qkl")
        b_stack = sem("b_stack")
        b_v = sem("b_v")
        b_vh = sem("b_vh")
        b_vl = sem("b_vl")
        b_s = sem("b_s")
        b_max = sem("b_max")
        b_dup = sem("b_dup")
        b_row = sem("b_row")
        b_rowh = sem("b_rowh")
        b_rowl = sem("b_rowl")
        b_st = sem("b_st")
        b_exp = sem("b_exp")
        b_eh = sem("b_eh")
        b_el = sem("b_el")
        b_pv = sem("b_pv")
        b_yinv = sem("b_yinv")
        b_yfac = sem("b_yfac")
        b_y = sem("b_y")
        b_out = sem("b_out")
        n_ = {k: {e: sem(f"{k}n_{e}") for e in (
            "tr",
            "xt",
            "bn",
            "mv",
            "gm",
            "gmc",
            "dev",
            "sq",
            "var",
            "gv",
            "ve",
            "r",
            "nb",
            "xn",
            "nh",
            "nl",
        )} for k in "ab"}
        bufs = {"a": dict(src=xin, xT=a_xT, xn=xn32[0], nh=a_nh, nl=a_nl, ps=pa, **norm["a"], **{"s_" + k: v for k, v in n_["a"].items()}),
                "b": dict(src=x1, xT=b_xTs, xn=xn32[0], nh=b_nh, nl=b_nl, ps=pb, **norm["b"], **{"s_" + k: v for k, v in n_["b"].items()})}

        def after(eng, s, value):
            if not (isinstance(value, int) and value <= 0):
                eng.wait_ge(s, value)

        def split3(out_ap, lhs, rhs, start=True, stop=True):
            (lh, ll), (rh, rl) = lhs, rhs
            nc.tensor.matmul(out_ap, lh, rh, start=start, stop=False)
            nc.tensor.matmul(out_ap, lh, rl, start=False, stop=False)
            return nc.tensor.matmul(out_ap, ll, rh, start=False, stop=stop)

        def out_banks(g):
            return pa[:].rearrange("p w (t g su i) -> p g (w t) su i", t=TILES, g=2, i=4)[:, g]

        def out_parts(part, g):
            return o_src[:].rearrange("p s u l g (n i) -> p l g n (s u) i", i=4)[:, part, g]

        block = ctx.enter_context(nc.Block())

        @block.sync
        def _(sp):
            sp.dma_start(ident[:], ident_d).then_inc(s_const, 16)
            sp.dma_start(group_avg[:], group_d).then_inc(s_const, 16)
            sp.dma_start(masks[:], masks_d).then_inc(s_const, 16)

            def load(b):
                for c in range(CHUNKS):
                    after(sp, n_["a"]["tr"], nth(b, 4, 0))
                    sp.nop(nofuse=True)
                    after(sp, a_xb, nth(b, 1, 0))
                    sp.nop(nofuse=True)
                    src = x_v[b] if isinstance(b, int) else x_v[bass.ds(b, 1)].rearrange("o t p c -> (o t) p c")
                    sp.dma_start(xin[:, c * TPC:(c + 1) * TPC, :],
                                 src[c * TPC:(c + 1) * TPC].rearrange("t p c -> p t c")).then_inc(a_load[c], 16)

            def b_stacks(b):
                sp.wait_ge(b_qkl, nth(b, 2, 2))
                sp.nop(nofuse=True)
                after(sp, b_st, nth(b, 8, 0))
                sp.nop(nofuse=True)
                sp.dma_start(q_stack[0:64, :], qk_hl[0:64, :]).then_inc(b_stack, 16)
                sp.dma_start(k_stack[32:96, :], qk_hl[64:128, :]).then_inc(b_stack, 16)
                sp.dma_start(q_stack[64:96, :], qk_hl[0:32, :]).then_inc(b_stack, 16)
                sp.dma_start(k_stack[0:32, :], qk_hl[64:96, :]).then_inc(b_stack, 16)

            def a_regroup(b):
                sp.wait_ge(a_ol, nth(b, 1, 1))
                sp.nop(nofuse=True)
                after(sp, a_y, nth(b, 4, 0))
                sp.nop(nofuse=True)
                for r in range(4):
                    for s in range(4):
                        sp.dma_start(o_dst[32 * s:32 * s + 32, r], o_src[32 * r:32 * r + 32, s]).then_inc(a_ox, 16)

            def store(b):
                dst = out_v[b] if isinstance(b, int) else out_v[bass.ds(b, 1)].rearrange("o t p c -> (o t) p c")
                for it in range(0, TILES, 2):
                    sp.wait_ge(b_y, nth(b, 8, it + 2))
                    sp.nop(nofuse=True)
                    sp.dma_start(dst[it:it + 2].rearrange("t p c -> p t c"), y[:, it:it + 2, :]).then_inc(b_out, 16)

            load(0)
            sp.dma_start(wqkv_f, w_qkv.rearrange("(a p) n -> p a n", p=P)).then_inc(s_w, 16)
            sp.dma_start(wp_f, w_proj.rearrange("(a p) n -> p a n", p=P)).then_inc(s_w, 16)
            for n, w in enumerate((wq1, wq1, wk1, wk1)):
                sp.dma_start(wqk1_f[:, :, n * 32:(n + 1) * 32], w.rearrange("(a p) n -> p a n", p=P)).then_inc(s_w, 16)
            sp.dma_start(wv1_f, wv1.rearrange("(a p) n -> p a n", p=P)).then_inc(s_w, 16)
            sp.dma_start(bias[:], b_proj.rearrange("(o n) -> o n", o=1).broadcast_to([P, CH])).then_inc(s_const, 16)
            sp.dma_start(gam[:], gamma.rearrange("(o n) -> o n", o=1).broadcast_to([P, 1])).then_inc(s_const, 16)
            load(1)
            a_regroup(0)
            load(2)
            b_stacks(0)
            a_regroup(1)
            load(3)
            store(0)
            with sp.Fori(1, IMAGES - 3) as i:
                b_stacks(i)
                a_regroup(i + 1)
                load(i + 3)
                store(i)
            for b in range(IMAGES - 3, IMAGES):
                b_stacks(b)
                if b + 1 < IMAGES:
                    a_regroup(b + 1)
                store(b)
            sp.wait_ge(b_out, nth(IMAGES, 64, 0))

        @block.tensor
        def _(pe):
            def transposes(k, b):
                u = bufs[k]
                for c in range(CHUNKS):
                    for ct in range(CT):
                        j = c * CT + ct
                        if k == "a":
                            pe.wait_ge(a_load[c], nth(b, 16, 16))
                            after(pe, a_ol, nth(b, 1, 0))
                            after(pe, a_x1, nth(b, 4, 0))
                        else:
                            pe.wait_ge(a_x1, nth(b, 4, 2 * (c + 1)))
                            after(pe, b_y, nth(b, 8, 0))
                        for t in range(TPC):
                            last = nc.tensor.transpose(u["ps"][:, j, t * P:(t + 1) * P],
                                                       u["src"][:, c * TPC + t, ct * P:(ct + 1) * P], ident[:])
                        last.then_inc(u["s_tr"], 1)

            def group_mean(k, b):
                u = bufs[k]
                pe.wait_ge(u["s_mv"], nth(b, 2, 2))
                nc.tensor.matmul(u["ps"][:, 0, 0:CT], group_avg[:], u["mv"][:, :, 0], start=True, stop=True).then_inc(u["s_gm"], 1)

            def group_var(k, b):
                u = bufs[k]
                pe.wait_ge(u["s_var"], nth(b, 1, 1))
                nc.tensor.matmul(u["ps"][:, 1, 0:CT], group_avg[:], u["e"][:], start=True, stop=True).then_inc(u["s_gv"], 1)

            def project_T(out_ap, wh, wl, cols, c, nh, nl):
                tok = slice(c * CHUNK, (c + 1) * CHUNK)
                for ct in range(CT):
                    last = split3(out_ap, (wh[:, ct, cols], wl[:, ct, cols]), (nh[:, ct, tok], nl[:, ct, tok]),
                                  start=(ct == 0), stop=(ct == CT - 1))
                return last

            def project(out_ap, lhs, wh, wl, cols):
                for ct in range(CT):
                    last = split3(out_ap, (lhs[0][:, ct], lhs[1][:, ct]), (wh[:, ct, cols], wl[:, ct, cols]),
                                  start=(ct == 0), stop=(ct == CT - 1))
                return last

            def a_project_qk(b, c):
                pe.wait_ge(n_["a"]["nl"], nth(b, 4, 2 * c + 2))
                for d in range(4):
                    if c:
                        pe.wait_ge(a_qke, nth(b, 8, d + 1))
                    project_T(pa[:, d, :], wqkv_h, wqkv_l, slice(d * P, (d + 1) * P), c, a_nh, a_nl).then_inc(a_qk, 1)

            def a_project_v(b):
                for j in range(4):
                    pe.wait_ge(a_qke, nth(b, 8, 5 + j))
                    for t in range(2):
                        tok = slice((2 * j + t) * P, (2 * j + t + 1) * P)
                        last = project(pa[:, j, t * CH:(t + 1) * CH], (a_nh[:, :, tok], a_nl[:, :, tok]),
                                       wqkv_h, wqkv_l, slice(2 * CH, 3 * CH))
                    last.then_inc(a_v, 1)

            def a_scores(b, c):
                pe.wait_ge(a_qke, nth(b, 8, 8))
                pe.wait_ge(a_ve, nth(b, 4, 4))
                if c:
                    pe.wait_ge(a_sub, nth(b, 2, c))
                pe.nop(nofuse=True)
                for t in range(TPC):
                    for g in range(2):
                        for w in range(4):
                            n = (c * TPC + t) * 4 + w
                            tok = slice(n * WIN, (n + 1) * WIN)
                            for r in range(4):
                                rows = slice(32 * r, 32 * r + 32)
                                col = (2 * t + g) * WIN
                                last = nc.tensor.matmul(pa[32 * w:32 * w + 32, r, col:col + WIN],
                                                        qkT[rows, g, tok], qkT[rows, 2 + g, tok], start=True, stop=True)
                last.then_inc(a_s, 1)

            def a_output(b):
                pe.wait_ge(a_pt, nth(b, 2, 2))
                pe.nop(nofuse=True)
                for t in range(TILES):
                    for g in range(2):
                        for r in range(4):
                            h = 4 * g + r
                            blk = (r * 8 + 2 * (t % TPC) + g) * WIN
                            for w in range(4):
                                rows = slice(32 * w, 32 * w + 32)
                                col = (2 * t + g) * WIN
                                last = nc.tensor.matmul(pa[32 * r:32 * r + 32, w, col:col + WIN], v_tok[rows, t, h * DH:(h + 1) * DH],
                                                        pT[rows, t // TPC, blk:blk + WIN], start=True, stop=True)
                last.then_inc(a_o, 1)

            def a_projection(b):
                pe.wait_ge(a_ox, nth(b, 256, 256))
                for j in range(4):
                    for t in range(2):
                        h = 2 * j + t
                        lhs = [o_dst[:, h % 4, :, part, h // 4, :] for part in (0, 1)]
                        last = project(pa[:, j, t * CH:(t + 1) * CH], lhs, wp_h, wp_l, slice(0, CH))
                    last.then_inc(a_y, 1)

            def b_project(b):
                for c in range(CHUNKS):
                    pe.wait_ge(n_["b"]["nl"], nth(b, 4, 2 * c + 2))
                    project_T(pb[:, 2 + c, :], wqk1_h, wqk1_l, slice(0, P), c, b_nh, b_nl).then_inc(b_qk, 1)
                for j in range(4):
                    if j >= 2:
                        pe.wait_ge(b_qkl, nth(b, 2, j - 1))
                    for t in range(2):
                        tok = slice((2 * j + t) * P, (2 * j + t + 1) * P)
                        last = project(pb[:, j, t * CH:(t + 1) * CH], (b_nh[:, :, tok], b_nl[:, :, tok]), wv1_h, wv1_l, slice(0, CH))
                    last.then_inc(b_v, 1)

            def b_energy(b, its):
                for it in its:
                    pe.wait_ge(b_stack, nth(b, 64, 64))
                    if it < 2:
                        pe.wait_ge(b_vl, nth(b, 4, 2 * it + 2))
                    else:
                        pe.wait_ge(b_max, nth(b, 8, it - 1))
                    for c in range(CHUNKS):
                        last = nc.tensor.matmul(pb[:, 2 * (it % 2) + c, :], k_stack[0:96, it * P:(it + 1) * P],
                                                q_stack[0:96, c * CHUNK:(c + 1) * CHUNK], start=True, stop=True)
                    last.then_inc(b_s, 1)

            def b_max_rows(b):
                pe.wait_ge(b_dup, nth(b, 1, 1))
                for it in range(TILES):
                    last = nc.tensor.matmul(pb[96:98, it // TPC, (it % TPC) * P:(it % TPC + 1) * P],
                                            max_dup[:, it, :], ident[:], start=True, stop=True)
                last.then_inc(b_row, 1)

            def b_energy_T(b, jts):
                for jt in jts:
                    pe.wait_ge(b_rowl, nth(b, 1, 1))
                    if jt >= 2:
                        pe.wait_ge(b_exp, nth(b, 8, jt - 1))
                    for c in range(CHUNKS):
                        last = nc.tensor.matmul(pb[:, 2 * (jt % 2) + c, :], q_stack[0:98, jt * P:(jt + 1) * P],
                                                k_stack[0:98, c * CHUNK:(c + 1) * CHUNK], start=True, stop=True)
                    last.then_inc(b_st, 1)

            def b_output(b, its):
                for it in its:
                    pe.wait_ge(b_el, nth(b, 8, 8))
                    if it >= 4:
                        pe.wait_ge(b_y, nth(b, 8, it - 3))
                    rows = slice(it * P, (it + 1) * P)
                    for jt in range(TILES):
                        last = split3(pb[:, it % 4, 0:CH + 1], (e_h[:, jt, rows], e_l[:, jt, rows]),
                                      (v_h[:, jt, 0:CH + 1], v_l[:, jt, 0:CH + 1]), start=(jt == 0), stop=(jt == TILES - 1))
                    last.then_inc(b_pv, 1)

            def step(b, m, f):
                if b is not None: transposes("b", b)
                if m is not None: a_project_qk(m, 0)
                if b is not None: group_mean("b", b)
                if m is not None: a_project_qk(m, 1)
                if b is not None: group_var("b", b)
                if m is not None: a_project_v(m)
                if b is not None: b_project(b)
                if m is not None: a_scores(m, 0)
                if b is not None: b_energy(b, range(0, 4))
                if m is not None: a_scores(m, 1)
                if b is not None: b_energy(b, range(4, 8))
                if b is not None: b_max_rows(b)
                if b is not None: b_energy_T(b, range(0, 4))
                if m is not None: a_output(m)
                if b is not None: b_energy_T(b, range(4, 8))
                if b is not None: b_output(b, range(0, 4))
                if m is not None: a_projection(m)
                if f is not None: transposes("a", f)
                if b is not None: b_output(b, range(4, 6))
                if f is not None: group_mean("a", f)
                if b is not None: b_output(b, range(6, 7))
                if f is not None: group_var("a", f)
                if b is not None: b_output(b, range(7, 8))

            pe.wait_ge(s_const, 80)
            transposes("a", 0)
            group_mean("a", 0)
            group_var("a", 0)
            pe.wait_ge(s_wmax, 1)
            nc.tensor.transpose(pb[0:5, 0, 0:P], wmax[:], ident[:]).then_inc(s_wmaxT, 1)
            pe.wait_ge(s_diag, 1)
            nc.tensor.matmul(pb[:, 1, 0:5], ones5[:], wmax_diag[:], start=True, stop=True).then_inc(s_unit_ps, 1)
            pe.wait_ge(s_ready, 1)
            step(None, 0, 1)
            step(0, 1, 2)
            with pe.Fori(1, IMAGES - 2) as i:
                step(i, i + 1, i + 2)
            step(IMAGES - 2, IMAGES - 1, None)
            step(IMAGES - 1, None, None)

        @block.scalar
        def _(act):
            def copy_T(k, b):
                u = bufs[k]
                for c in range(CHUNKS):
                    for ct in range(CT):
                        j = c * CT + ct
                        act.wait_ge(u["s_tr"], nth(b, 4, j + 1))
                        nc.scalar.activation(u["xT"][:, ct, c * CHUNK:(c + 1) * CHUNK], u["ps"][:, j, :], ACT.Copy).then_inc(u["s_xt"], 1)

            def normalise(k, b, last):
                u = bufs[k]
                act.wait_ge(u["s_nb"], nth(b, 1, 1))
                for c in range(CHUNKS):
                    for ct in range(CT):
                        j = c * CT + ct
                        if last is not None:
                            act.wait_ge(n_[last[0]]["nl"], nth(last[1], 4, j + 1))
                        if k == "a":
                            src = u["xT"][:, ct, :].rearrange("p (w t k) -> p t w k", w=4, k=WIN)[:, c * TPC:(c + 1) * TPC]
                            dst = u["xn"][:, j, :].rearrange("p (t w k) -> p t w k", w=4, k=WIN)
                        else:
                            src, dst = u["xT"][:, ct, c * CHUNK:(c + 1) * CHUNK], u["xn"][:, j, :]
                        nc.scalar.activation(dst, src, ACT.Identity,
                                             scale=u["r"][:, ct:ct + 1], bias=u["nb"][:, ct:ct + 1]).then_inc(u["s_xn"], 1)

            def a_copy_qk(b, c):
                for d in range(4):
                    act.wait_ge(a_qk, nth(b, 8, 4 * c + d + 1))
                    dst = qkT[:, d, c * CHUNK:(c + 1) * CHUNK]
                    after(act, a_s, nth(b, 2, 0))
                    if d < 2:
                        for u in range(2):
                            last = nc.scalar.activation(dst.rearrange("p (n s u i) -> p u n s i", s=4, u=2, i=4)[:, u],
                                                        pa[:, d, :].rearrange("p (n i u s) -> p u n s i", s=4, u=2, i=4)[:, u],
                                                        ACT.Copy, scale=f_q[:, 0:1])
                        last.then_inc(a_qke, 1)
                    else:
                        nc.scalar.activation(dst, pa[:, d, :], ACT.Copy).then_inc(a_qke, 1)

            def a_copy_v(b):
                for j in range(4):
                    act.wait_ge(a_v, nth(b, 4, j + 1))
                    after(act, a_o, nth(b, 1, 0))
                    nc.scalar.activation(v_tok[:, 2 * j:2 * j + 2, :].rearrange("p t n -> p (t n)"), pa[:, j, :], ACT.Copy).then_inc(a_ve, 1)

            def a_exponential(b, c):
                act.wait_ge(a_sub, nth(b, 2, c + 1))
                nc.scalar.activation(s32[:, c, :], s32[:, c, :], ACT.Exp).then_inc(a_exp, 1)

            def a_out_high(b):
                act.wait_ge(a_o, nth(b, 1, 1))
                after(act, a_ox, nth(b, 256, 0))
                for g in range(2):
                    last = nc.scalar.activation(out_parts(0, g), out_banks(g), ACT.Copy)
                last.then_inc(a_oh, 1)

            def b_qk_high(b):
                for c in range(CHUNKS):
                    act.wait_ge(b_qk, nth(b, 2, c + 1))
                    nc.scalar.activation(qk_h[:, c * CHUNK:(c + 1) * CHUNK], pb[:, 2 + c, :], ACT.Copy).then_inc(b_qkh, 1)

            def b_v_high(b):
                for j in range(4):
                    act.wait_ge(b_v, nth(b, 4, j + 1))
                    after(act, b_pv, nth(b, 8, 0))
                    nc.scalar.activation(v_h[:, 2 * j:2 * j + 2, 0:CH], pb[:, j, :].rearrange("p (t n) -> p t n", t=2), ACT.Copy).then_inc(b_vh, 1)

            def b_row_high(b):
                act.wait_ge(b_row, nth(b, 1, 1))
                nc.scalar.activation(max_row[96:98, :], pb[96:98, 0:2, :].rearrange("p a n -> p (a n)"), ACT.Copy).then_inc(b_rowh, 1)

            def b_exponential(b, jts):
                for jt in jts:
                    act.wait_ge(b_st, nth(b, 8, jt + 1))
                    after(act, b_el, nth(b, 8, jt - 1) if jt >= 2 else nth(b, 8, 0))
                    nc.scalar.activation(e32[:, jt % 2, :], pb[:, 2 * (jt % 2):2 * (jt % 2) + 2, :].rearrange("p a n -> p (a n)"),
                                         ACT.Exp, scale=f_energy[:, 0:1]).then_inc(b_exp, 1)

            def step(b, m, f):
                if b is not None: copy_T("b", b)
                if m is not None: a_copy_qk(m, 0)
                if m is not None: a_copy_qk(m, 1)
                if b is not None: normalise("b", b, ("a", b + 1) if m is not None else ("b", b - 1))
                if m is not None: a_copy_v(m)
                if b is not None: b_qk_high(b)
                if b is not None: b_v_high(b)
                if m is not None: a_exponential(m, 0)
                if m is not None: a_exponential(m, 1)
                if b is not None: b_row_high(b)
                if b is not None: b_exponential(b, range(0, 4))
                if m is not None: a_out_high(m)
                if b is not None: b_exponential(b, range(4, 8))
                if f is not None: copy_T("a", f)
                if f is not None: normalise("a", f, ("b", b) if b is not None else ("a", f - 1))

            copy_T("a", 0)
            normalise("a", 0, None)
            act.wait_ge(s_ready, 1)
            step(None, 0, 1)
            step(0, 1, 2)
            with act.Fori(1, IMAGES - 2) as i:
                step(i, i + 1, i + 2)
            step(IMAGES - 2, IMAGES - 1, None)
            step(IMAGES - 1, None, None)

        @block.vector
        def _(dve):
            def stats(k, b):
                u = bufs[k]
                for c in range(CHUNKS):
                    for ct in range(CT):
                        dve.wait_ge(u["s_xt"], nth(b, 4, c * CT + ct + 1))
                        nc.vector.bn_stats(u["st"][:, ct, c, :], u["xT"][:, ct, c * CHUNK:(c + 1) * CHUNK]).then_inc(u["s_bn"], 1)
                dve.wait_ge(u["s_bn"], nth(b, 4, 4))
                dve.nop(nofuse=True)
                for ct in range(CT):
                    nc.vector.bn_aggr(u["mv"][:, ct, :], u["st"][:, ct].rearrange("p c s -> p (c s)")).then_inc(u["s_mv"], 1)

            def group_mean(k, b):
                u = bufs[k]
                dve.wait_ge(u["s_gm"], nth(b, 1, 1))
                nc.vector.tensor_scalar(u["gm"][:], u["ps"][:, 0, 0:CT], -1.0, None, ALU.mult).then_inc(u["s_gmc"], 1)
                dve.wait_ge(u["s_gmc"], nth(b, 1, 1))
                nc.vector.tensor_tensor(u["d"][:], u["mv"][:, :, 0], u["gm"][:], ALU.add).then_inc(u["s_dev"], 1)
                dve.wait_ge(u["s_dev"], nth(b, 1, 1))
                nc.vector.tensor_tensor(u["e"][:], u["d"][:], u["d"][:], ALU.mult).then_inc(u["s_sq"], 1)
                dve.wait_ge(u["s_sq"], nth(b, 1, 1))
                nc.vector.tensor_tensor(u["e"][:], u["e"][:], u["mv"][:, :, 1], ALU.add).then_inc(u["s_var"], 1)

            def group_scale(k, b):
                u = bufs[k]
                dve.wait_ge(u["s_gv"], nth(b, 1, 1))
                nc.vector.tensor_scalar(u["ve"][:], u["ps"][:, 1, 0:CT], EPS, None, ALU.add).then_inc(u["s_ve"], 1)

            def norm_high(k, b):
                u = bufs[k]
                for c in range(CHUNKS):
                    for ct in range(CT):
                        j = c * CT + ct
                        dve.wait_ge(u["s_xn"], nth(b, 4, j + 1))
                        after(dve, a_v if k == "a" else b_v, nth(b, 4, 0))
                        nc.vector.tensor_copy(u["nh"][:, ct, c * CHUNK:(c + 1) * CHUNK], u["xn"][:, j, :]).then_inc(u["s_nh"], 1)

            heads4 = dict(n=8, k=WIN)

            def a_maximum(b, c):
                dve.wait_ge(a_s, nth(b, 2, c + 1))
                s = pa[:, :, 0:CH].rearrange("p r (n k) -> p r n k", **heads4)
                m = a_rmax[:, c, :].rearrange("p (r n) -> p r n", r=4)
                nc.vector.tensor_reduce(m, s, X, ALU.max).then_inc(a_max, 1)
                dve.wait_ge(a_max, nth(b, 2, c + 1))
                nc.vector.tensor_tensor(s32[:, c, :].rearrange("p (r n k) -> p r n k", r=4, k=WIN), s,
                                        m.unsqueeze(3).broadcast_to([P, 4, 8, WIN]), ALU.subtract).then_inc(a_sub, 1)

            def a_row_sum(b, c):
                dve.wait_ge(a_exp, nth(b, 2, c + 1))
                nc.vector.tensor_reduce(a_rsum[:, c, :], s32[:, c, :].rearrange("p (n k) -> p n k", k=WIN), X, ALU.add).then_inc(a_sum, 1)
                dve.wait_ge(a_sum, nth(b, 2, c + 1))
                nc.vector.reciprocal(a_rinv[:, c, :], a_rsum[:, c, :]).then_inc(a_inv, 1)

            def a_transpose(b, c):
                dve.wait_ge(a_prob, nth(b, 2, c + 1))
                after(dve, a_o, nth(b, 1, 0))
                nc.vector.transpose(pT[:, c, :], s32[:, c, :]).then_inc(a_pt, 1)

            def a_out_low(b):
                dve.wait_ge(a_oh, nth(b, 1, 1))
                for g in range(2):
                    last = nc.vector.tensor_tensor(out_parts(1, g), out_banks(g), out_parts(0, g), ALU.subtract)
                last.then_inc(a_ol, 1)

            def a_residual(b):
                dve.wait_ge(a_xb, nth(b, 1, 1))
                after(dve, n_["b"]["tr"], nth(b, 4, 0))
                after(dve, b_copy, nth(b, 1, 0))
                for j in range(4):
                    dve.wait_ge(a_y, nth(b, 4, j + 1))
                    nc.vector.scalar_tensor_tensor(x1[:, 2 * j:2 * j + 2, :].rearrange("p t n -> p (t n)"), pa[:, j, :], f_proj[:, 0:1],
                                                   xb[:, 2 * j:2 * j + 2, :].rearrange("p t n -> p (t n)"), ALU.mult, ALU.add).then_inc(a_x1, 1)

            def b_qk_low(b):
                after(dve, b_stack, nth(b, 64, 0))
                for c in range(CHUNKS):
                    dve.wait_ge(b_qkh, nth(b, 2, c + 1))
                    cols = slice(c * CHUNK, (c + 1) * CHUNK)
                    nc.vector.scalar_tensor_tensor(qk_hl[:, cols], qk_h[:, cols], masks[:, 0:1], pb[:, 2 + c, :],
                                                   ALU.mult, ALU.add).then_inc(b_qkl, 1)

            def b_v_low(b):
                for j in range(4):
                    dve.wait_ge(b_vh, nth(b, 4, j + 1))
                    nc.vector.tensor_tensor(v_l[:, 2 * j:2 * j + 2, 0:CH], pb[:, j, :].rearrange("p (t n) -> p t n", t=2),
                                            v_h[:, 2 * j:2 * j + 2, 0:CH], ALU.subtract).then_inc(b_vl, 1)

            def b_maximum(b, its):
                for it in its:
                    dve.wait_ge(b_s, nth(b, 8, it + 1))
                    nc.vector.tensor_reduce(max_neg[:, it:it + 1], pb[:, 2 * (it % 2):2 * (it % 2) + 2, :].rearrange("p a n -> p (a n)"),
                                            X, ALU.max, negate=True).then_inc(b_max, 1)

            def b_duplicate(b):
                dve.wait_ge(b_max, nth(b, 8, 8))
                nc.vector.tensor_scalar(max_dup[:], max_neg[:].unsqueeze(2).broadcast_to([P, TILES, 2]),
                                        1.0 / ROW_SCALE, None, ALU.mult).then_inc(b_dup, 1)

            def b_row_low(b):
                dve.wait_ge(b_rowh, nth(b, 1, 1))
                nc.vector.scalar_tensor_tensor(k_stack[96:98, :], max_row[96:98, :], masks[96:98, 1:2],
                                               pb[96:98, 0:2, :].rearrange("p a n -> p (a n)"), ALU.mult, ALU.add).then_inc(b_rowl, 1)

            def b_split(b, jts):
                for jt in jts:
                    dve.wait_ge(b_exp, nth(b, 8, jt + 1))
                    nc.vector.tensor_copy(e_h[:, jt, :], e32[:, jt % 2, :]).then_inc(b_eh, 1)
                    dve.wait_ge(b_eh, nth(b, 8, jt + 1))
                    nc.vector.tensor_tensor(e_l[:, jt, :], e32[:, jt % 2, :], e_h[:, jt, :], ALU.subtract).then_inc(b_el, 1)

            def b_result(b, its):
                dve.wait_ge(b_copy, nth(b, 1, 1))
                for it in its:
                    dve.wait_ge(b_pv, nth(b, 8, it + 1))
                    nc.vector.reciprocal(y_inv[:, it:it + 1], pb[:, it % 4, CH:CH + 1]).then_inc(b_yinv, 1)
                    dve.wait_ge(b_yinv, nth(b, 8, it + 1))
                    nc.vector.tensor_tensor(y_fac[:, it:it + 1], y_inv[:, it:it + 1], f_out[:, 0:1], ALU.mult).then_inc(b_yfac, 1)
                    dve.wait_ge(b_yfac, nth(b, 8, it + 1))
                    nc.vector.scalar_tensor_tensor(y[:, it, :], pb[:, it % 4, 0:CH], y_fac[:, it:it + 1], y[:, it, :],
                                                   ALU.mult, ALU.add).then_inc(b_y, 1)

            def step(b, m, f):
                if b is not None: stats("b", b)
                if b is not None: group_mean("b", b)
                if b is not None: group_scale("b", b)
                if b is not None: norm_high("b", b)
                if b is not None: b_qk_low(b)
                if b is not None: b_v_low(b)
                if m is not None: a_maximum(m, 0)
                if b is not None: b_maximum(b, range(0, 4))
                if m is not None: a_row_sum(m, 0)
                if m is not None: a_maximum(m, 1)
                if b is not None: b_maximum(b, range(4, 8))
                if b is not None: b_duplicate(b)
                if m is not None: a_row_sum(m, 1)
                if m is not None: a_transpose(m, 0)
                if b is not None: b_row_low(b)
                if b is not None: b_split(b, range(0, 1))
                if m is not None: a_transpose(m, 1)
                if b is not None: b_split(b, range(1, 8))
                if m is not None: a_out_low(m)
                if b is not None: b_result(b, range(0, 4))
                if m is not None: a_residual(m)
                if f is not None: stats("a", f)
                if f is not None: group_mean("a", f)
                if b is not None: b_result(b, range(4, 6))
                if f is not None: group_scale("a", f)
                if f is not None: norm_high("a", f)
                if b is not None: b_result(b, range(6, 8))

            chain = [0]

            def link(ins):
                chain[0] += 1
                ins.then_inc(s_chain, 1)
                dve.wait_ge(s_chain, chain[0])

            stats("a", 0)
            group_mean("a", 0)
            group_scale("a", 0)
            norm_high("a", 0)
            dve.wait_ge(s_const, 80)
            dve.wait_ge(s_w, 112)
            for n, w in enumerate((wqkv_f, wp_f, wqk1_f[:, :, 0:32], wqk1_f[:, :, 64:96], wv1_f)):
                last = nc.vector.tensor_reduce(wmax[:, n:n + 1], w, mybir.AxisListType.XY, ALU.max, apply_absolute_value=True)
            last.then_inc(s_wmax, 1)
            dve.wait_ge(s_wmaxT, 1)
            link(nc.vector.tensor_reduce(wmax_all[:], pb[0:5, 0, 0:P], X, ALU.max))
            link(nc.vector.tensor_scalar(wmax_all[:], wmax_all[:], 1e-30, 2.0, ALU.max, ALU.mult))
            link(nc.vector.memset(ones5[:], 1.0))
            nc.vector.tensor_scalar(wmax_diag[:], ident[0:5, 0:5], wmax_all[:, 0:1], None, ALU.mult).then_inc(s_diag, 1)
            dve.wait_ge(s_unit_ps, 1)
            link(nc.vector.tensor_copy(unit[:], pb[:, 1, 0:5]))
            link(nc.vector.reciprocal(unit_inv[:], unit[:]))
            link(nc.vector.scalar_tensor_tensor(f_q[:], unit[:, 0:1], DH ** -0.5, unit[:, 0:1], ALU.mult, ALU.mult))
            link(nc.vector.tensor_tensor(f_proj[:], unit[:, 0:1], unit[:, 1:2], ALU.mult))
            link(nc.vector.tensor_tensor(f_energy[:], unit[:, 2:3], unit[:, 3:4], ALU.mult))
            link(nc.vector.tensor_tensor(f_out[:], unit[:, 4:5], gam[:], ALU.mult))
            for w, n in ((wqkv_f, 0), (wp_f, 1), (wqk1_f[:, :, 0:64], 2), (wqk1_f[:, :, 64:128], 3), (wv1_f, 4)):
                link(nc.vector.tensor_scalar(w, w, unit_inv[:, n:n + 1], None, ALU.mult))
            for f, h, l in weights:
                link(nc.vector.tensor_copy(h[:], f))
            for f, h, l in weights:
                last = nc.vector.tensor_tensor(l[:], f, h[:], ALU.subtract)
            dve.wait_ge(s_pool, 5)
            last.then_inc(s_ready, 1)
            step(None, 0, 1)
            step(0, 1, 2)
            with dve.Fori(1, IMAGES - 2) as i:
                step(i, i + 1, i + 2)
            step(IMAGES - 2, IMAGES - 1, None)
            step(IMAGES - 1, None, None)

        @block.gpsimd
        def _(pool):
            def rstd(k, b):
                u = bufs[k]
                pool.wait_ge(u["s_ve"], nth(b, 1, 1))
                nc.gpsimd.tensor_tensor(u["r"][:], u["ve"][:], minus_half[:], ALU.pow).then_inc(u["s_r"], 1)
                pool.wait_ge(u["s_r"], nth(b, 1, 1))
                nc.gpsimd.tensor_tensor(u["nb"][:], u["gm"][:], u["r"][:], ALU.mult).then_inc(u["s_nb"], 1)

            def norm_low(k, b):
                u = bufs[k]
                for c in range(CHUNKS):
                    for ct in range(CT):
                        j = c * CT + ct
                        cols = slice(c * CHUNK, (c + 1) * CHUNK)
                        pool.wait_ge(u["s_nh"], nth(b, 4, j + 1))
                        nc.gpsimd.tensor_tensor(u["nl"][:, ct, cols], u["xn"][:, j, :], u["nh"][:, ct, cols], ALU.subtract).then_inc(u["s_nl"], 1)

            def add_bias(b):
                for c in range(CHUNKS):
                    pool.wait_ge(a_load[c], nth(b, 16, 16))
                after(pool, a_x1, nth(b, 4, 0))
                nc.gpsimd.tensor_tensor(xb[:], xin[:], bias[:].unsqueeze(1).broadcast_to([P, TILES, CH]), ALU.add).then_inc(a_xb, 1)

            def a_probabilities(b, c):
                pool.wait_ge(a_inv, nth(b, 2, c + 1))
                v = s32[:, c, :].rearrange("p (n k) -> p n k", k=WIN)
                nc.gpsimd.tensor_tensor(v, v, a_rinv[:, c, :].unsqueeze(2).broadcast_to([P, 32, WIN]), ALU.mult).then_inc(a_prob, 1)

            def b_keep(b):
                pool.wait_ge(a_x1, nth(b, 4, 4))
                after(pool, b_out, nth(b, 64, 0))
                pool.nop(nofuse=True)
                nc.gpsimd.tensor_copy(y[:], x1[:]).then_inc(b_copy, 1)

            def step(b, m, f):
                if b is not None: b_keep(b)
                if b is not None: rstd("b", b)
                if b is not None: norm_low("b", b)
                if m is not None: a_probabilities(m, 0)
                if m is not None: a_probabilities(m, 1)
                if f is not None: add_bias(f)
                if f is not None: rstd("a", f)
                if f is not None: norm_low("a", f)

            nc.gpsimd.memset(q_stack[96:128, :], ROW_SCALE).then_inc(s_pool, 1)
            pool.wait_ge(s_pool, 1)
            nc.gpsimd.memset(k_stack[96:128, :], 0.0).then_inc(s_pool, 1)
            pool.wait_ge(s_pool, 2)
            nc.gpsimd.memset(v_h[:, :, CH:VCOL], 1.0).then_inc(s_pool, 1)
            nc.gpsimd.memset(v_l[:, :, CH:VCOL], 0.0).then_inc(s_pool, 1)
            nc.gpsimd.memset(minus_half[:], -0.5).then_inc(s_pool, 1)
            pool.wait_ge(s_pool, 5)
            pool.wait_ge(s_const, 80)
            add_bias(0)
            rstd("a", 0)
            norm_low("a", 0)
            step(None, 0, 1)
            step(0, 1, 2)
            with pool.Fori(1, IMAGES - 2) as i:
                step(i, i + 1, i + 2)
            step(IMAGES - 2, IMAGES - 1, None)
            step(IMAGES - 1, None, None)


_INS = ["x", "L0_conv_w_qkv", "L0_conv_w_proj", "L0_conv_b_proj", "L1_conv_Wq", "L1_conv_Wk", "L1_conv_Wv", "L1_conv_gamma"]


def kernel(**inputs):
    import numpy as _np
    import concourse.bacc as _bacc
    from concourse import mybir as _mybir
    from concourse.bass_utils import run_bass_kernel_spmd as _run

    nc = _bacc.Bacc("TRN2", target_bir_lowering=False, num_devices=1)
    arrays = {f"in_{name}": _np.ascontiguousarray(inputs[name]) for name in _INS}
    n = _np.arange(P)
    arrays["in_ident"] = _np.eye(P, dtype=_np.float32)
    arrays["in_group"] = _np.kron(_np.eye(P // GROUP), _np.full((GROUP, GROUP), 1.0 / GROUP)).astype(_np.float32)
    masks = _np.zeros((P, 2), _np.float32)
    masks[32:64, 0] = masks[96:128, 0] = -1.0
    masks[97, 1] = -1.0
    arrays["in_masks"] = masks
    args = [nc.dram_tensor(name, a.shape, _mybir.dt.from_np(a.dtype), kind="ExternalInput").ap() for name, a in arrays.items()]
    out = nc.dram_tensor("out_0", (IMAGES, 32, 32, CH), _mybir.dt.float32, kind="ExternalOutput").ap()
    build(nc, *args, out)
    r = _run(nc, [arrays], core_ids=[0])
    return r.results[0]["out_0"]
```

```python
import concourse.bass as bass
from concourse import mybir
from contextlib import ExitStack

F32 = mybir.dt.float32
F16 = mybir.dt.float16
ALU = mybir.AluOpType
ACT = mybir.ActivationFunctionType
X = mybir.AxisListType.X

P = 128
IMAGES, TOKENS, CH = 8, 1024, 256
TILES = TOKENS // P
CT = CH // P
CHUNK = 512
CHUNKS = TOKENS // CHUNK
TPC = CHUNK // P
HEADS, DH = 8, 32
WIN = 32
GROUP = 8
VCOL = CH + 2
EPS = 1e-5
ROW_SCALE = 2.0 ** 15


def nth(b, per, n):
    return b * per + n


def build(nc, x, w_qkv, w_proj, b_proj, wq1, wk1, wv1, gamma, ident_d, group_d, masks_d, out):
    x_v = x.rearrange("b (t y) w c -> b t (y w) c", t=TILES)
    out_v = out.rearrange("b (t y) w c -> b t (y w) c", t=TILES)

    with ExitStack() as ctx:
        def sb(name, shape, dt=F32):
            return ctx.enter_context(nc.sbuf_tensor(name, shape, dt))

        def sem(name):
            return ctx.enter_context(nc.semaphore(name))

        ident = sb("ident", [P, P])
        group_avg = sb("group_avg", [P, P])
        masks = sb("masks", [P, 2])
        bias = sb("bias", [P, CH])
        gam = sb("gam", [P, 1])
        wqkv_h, wqkv_l = sb("wqkv_h", [P, CT, 3 * CH], F16), sb("wqkv_l", [P, CT, 3 * CH], F16)
        wp_h, wp_l = sb("wp_h", [P, CT, CH], F16), sb("wp_l", [P, CT, CH], F16)
        wqk1_h, wqk1_l = sb("wqk1_h", [P, CT, P], F16), sb("wqk1_l", [P, CT, P], F16)
        wv1_h, wv1_l = sb("wv1_h", [P, CT, CH], F16), sb("wv1_l", [P, CT, CH], F16)
        wmax = sb("wmax", [P, 5])
        wmax_all = sb("wmax_all", [5, 1])
        wmax_diag = sb("wmax_diag", [5, 5])
        ones5 = sb("ones5", [5, P])
        unit = sb("unit", [P, 5])
        unit_inv = sb("unit_inv", [P, 5])
        f_q = sb("f_q", [P, 1])
        f_proj = sb("f_proj", [P, 1])
        f_energy = sb("f_energy", [P, 1])
        f_out = sb("f_out", [P, 1])
        minus_half = sb("minus_half", [P, CT])
        xin = sb("xin", [P, TILES, CH])
        xb = sb("xb", [P, TILES, CH])
        x1 = sb("x1", [P, TILES, CH])
        a_xT = sb("a_xT", [P, CT, TOKENS])
        xn32 = [sb(f"xn32_{n}", [P, CHUNKS * CT, CHUNK]) for n in range(1)]
        a_nh, a_nl = sb("a_nh", [P, CT, TOKENS], F16), sb("a_nl", [P, CT, TOKENS], F16)
        qkT = sb("qkT", [P, 4, TOKENS])
        v_tok = sb("v_tok", [P, TILES, CH])
        s32 = sb("s32", [P, CHUNKS, TPC * CH])
        pT = sb("pT", [P, CHUNKS, TPC * CH])
        o_src = sb("o_src", [P, 4, 2, 2, 2, P], F16)
        o_dst = sb("o_dst", [P, 4, 2, 2, 2, P], F16)
        a_rmax, a_rsum = sb("a_rmax", [P, CHUNKS, 32]), sb("a_rsum", [P, CHUNKS, 32])
        a_rinv = sb("a_rinv", [P, CHUNKS, 32])
        y = sb("y", [P, TILES, CH])
        b_xT = a_xT
        b_nh, b_nl = sb("b_nh", [P, CT, TOKENS], F16), sb("b_nl", [P, CT, TOKENS], F16)
        b_xTs = sb("b_xTs", [P, CT, TOKENS])
        qk_h = sb("qk_h", [P, TOKENS], F16)
        qk_hl = sb("qk_hl", [P, TOKENS], F16)
        q_stack = sb("q_stack", [P, TOKENS], F16)
        k_stack = sb("k_stack", [P, TOKENS], F16)
        v_h, v_l = sb("v_h", [P, TILES, VCOL], F16), sb("v_l", [P, TILES, VCOL], F16)
        max_neg = sb("max_neg", [P, TILES])
        max_dup = sb("max_dup", [P, TILES, 2])
        max_row = qk_h
        e32 = sb("e32", [P, 2, TOKENS])
        e_h, e_l = sb("e_h", [P, TILES, TOKENS], F16), sb("e_l", [P, TILES, TOKENS], F16)
        y_inv = sb("y_inv", [P, TILES])
        y_fac = sb("y_fac", [P, TILES])
        norm = {k: dict(st=sb(k + "st", [P, CT, CHUNKS, 6]), mv=sb(k + "mv", [P, CT, 2]),
                        gm=sb(k + "gm", [P, CT]), d=sb(k + "d", [P, CT]), e=sb(k + "e", [P, CT]),
                        ve=sb(k + "ve", [P, CT]), r=sb(k + "r", [P, CT]), nb=sb(k + "nb", [P, CT])) for k in "ab"}
        stage = e_l[:].rearrange("p t n -> p (t n)").bitcast(F32)
        wqkv_f = stage[:, 0:1536].rearrange("p (a n) -> p a n", a=CT)
        wp_f = stage[:, 1536:2048].rearrange("p (a n) -> p a n", a=CT)
        wqk1_f = stage[:, 2048:2304].rearrange("p (a n) -> p a n", a=CT)
        wv1_f = stage[:, 2304:2816].rearrange("p (a n) -> p a n", a=CT)
        weights = [(wqkv_f, wqkv_h, wqkv_l), (wp_f, wp_h, wp_l), (wqk1_f, wqk1_h, wqk1_l), (wv1_f, wv1_h, wv1_l)]

        pa = ctx.enter_context(nc.psum_tensor("pa", [P, 4, CHUNK], F32))
        pb = ctx.enter_context(nc.psum_tensor("pb", [P, 4, CHUNK], F32))

        s_const, s_w, s_chain = sem("s_const"), sem("s_w"), sem("s_chain")
        s_wmax, s_wmaxT, s_diag, s_unit_ps, s_ready = sem("s_wmax"), sem("s_wmaxT"), sem("s_diag"), sem("s_unit_ps"), sem("s_ready")
        s_pool = sem("s_pool")
        a_load = [sem(f"a_load{c}") for c in range(CHUNKS)]
        a_xb = sem("a_xb")
        a_x1 = sem("a_x1")
        a_s = sem("a_s")
        a_o = sem("a_o")
        a_y = sem("a_y")
        a_qk = sem("a_qk")
        a_v = sem("a_v")
        a_qke = sem("a_qke")
        a_ve = sem("a_ve")
        a_max = sem("a_max")
        a_sub = sem("a_sub")
        a_exp = sem("a_exp")
        a_sum = sem("a_sum")
        a_inv = sem("a_inv")
        a_prob = sem("a_prob")
        a_pt = sem("a_pt")
        a_oh = sem("a_oh")
        a_ol = sem("a_ol")
        a_ox = sem("a_ox")
        b_copy = sem("b_copy")
        b_qk = sem("b_qk")
        b_qkh = sem("b_qkh")
        b_qkl = sem("b_qkl")
        b_stack = sem("b_stack")
        b_v = sem("b_v")
        b_vh = sem("b_vh")
        b_vl = sem("b_vl")
        b_s = sem("b_s")
        b_max = sem("b_max")
        b_dup = sem("b_dup")
        b_row = sem("b_row")
        b_rowh = sem("b_rowh")
        b_rowl = sem("b_rowl")
        b_st = sem("b_st")
        b_exp = sem("b_exp")
        b_eh = sem("b_eh")
        b_el = sem("b_el")
        b_pv = sem("b_pv")
        b_yinv = sem("b_yinv")
        b_yfac = sem("b_yfac")
        b_y = sem("b_y")
        b_out = [sem(f"b_out{j}") for j in range(4)]
        n_ = {k: {e: sem(f"{k}n_{e}") for e in (
            "tr",
            "xt",
            "bn",
            "mv",
            "gm",
            "gmc",
            "dev",
            "sq",
            "var",
            "gv",
            "ve",
            "r",
            "nb",
            "xn",
            "nh",
            "nl",
        )} for k in "ab"}
        bufs = {"a": dict(src=xin, xT=a_xT, xn=xn32[0], nh=a_nh, nl=a_nl, ps=pa, bank=0, **norm["a"], **{"s_" + k: v for k, v in n_["a"].items()}),
                "b": dict(src=x1, xT=b_xTs, xn=xn32[0], nh=b_nh, nl=b_nl, ps=pb, bank=2, **norm["b"], **{"s_" + k: v for k, v in n_["b"].items()})}

        def after(eng, s, value):
            if not (isinstance(value, int) and value <= 0):
                eng.wait_ge(s, value)

        def all_steps(eng, step):
            def peeled(i):
                step(i, *(0 <= n < IMAGES for n in (i, i - 1, i + 1, i + 2)))
            for i in range(-2, 2):
                peeled(i)
            with eng.Fori(2, IMAGES - 3) as i:
                step(i, True, True, True, True)
            for i in range(IMAGES - 3, IMAGES + 1):
                peeled(i)

        def split3(out_ap, lhs, rhs, start=True, stop=True):
            (lh, ll), (rh, rl) = lhs, rhs
            nc.tensor.matmul(out_ap, lh, rh, start=start, stop=False)
            nc.tensor.matmul(out_ap, lh, rl, start=False, stop=False)
            return nc.tensor.matmul(out_ap, ll, rh, start=False, stop=stop)

        def out_banks(g):
            return pa[:].rearrange("p w (t g su i) -> p g (w t) su i", t=TILES, g=2, i=4)[:, g]

        def out_parts(part, g):
            return o_src[:].rearrange("p s u l g (n i) -> p l g n (s u) i", i=4)[:, part, g]

        block = ctx.enter_context(nc.Block())

        @block.sync
        def _(sp):
            sp.dma_start(ident[:], ident_d).then_inc(s_const, 16)
            sp.dma_start(group_avg[:], group_d).then_inc(s_const, 16)
            sp.dma_start(masks[:], masks_d).then_inc(s_const, 16)

            def load(b):
                for c in range(CHUNKS):
                    after(sp, n_["a"]["tr"], nth(b, 4, 0))
                    sp.nop(nofuse=True)
                    after(sp, a_xb, nth(b, 1, 0))
                    sp.nop(nofuse=True)
                    src = x_v[b] if isinstance(b, int) else x_v[bass.ds(b, 1)].rearrange("o t p c -> (o t) p c")
                    sp.dma_start(xin[:, c * TPC:(c + 1) * TPC, :],
                                 src[c * TPC:(c + 1) * TPC].rearrange("t p c -> p t c")).then_inc(a_load[c], 16)

            def b_stacks(b):
                sp.wait_ge(b_qkl, nth(b, 2, 2))
                sp.nop(nofuse=True)
                after(sp, b_st, nth(b, 8, 0))
                sp.nop(nofuse=True)
                sp.dma_start(q_stack[0:64, :], qk_hl[0:64, :]).then_inc(b_stack, 16)
                sp.dma_start(k_stack[32:96, :], qk_hl[64:128, :]).then_inc(b_stack, 16)
                sp.dma_start(q_stack[64:96, :], qk_hl[0:32, :]).then_inc(b_stack, 16)
                sp.dma_start(k_stack[0:32, :], qk_hl[64:96, :]).then_inc(b_stack, 16)

            def a_regroup(b):
                sp.wait_ge(a_ol, nth(b, 1, 1))
                sp.nop(nofuse=True)
                after(sp, a_y, nth(b, 4, 0))
                sp.nop(nofuse=True)
                for r in range(4):
                    for s in range(4):
                        sp.dma_start(o_dst[32 * s:32 * s + 32, r], o_src[32 * r:32 * r + 32, s]).then_inc(a_ox, 16)

            def store(b, j):
                dst = out_v[b] if isinstance(b, int) else out_v[bass.ds(b, 1)].rearrange("o t p c -> (o t) p c")
                sp.wait_ge(b_y, nth(b, 8, 2 * j + 2))
                sp.nop(nofuse=True)
                sp.dma_start(dst[2 * j:2 * j + 2].rearrange("t p c -> p t c"), y[:, 2 * j:2 * j + 2, :]).then_inc(b_out[j], 16)

            def step(i, b, o, m, f):
                for j in range(3):
                    if o: store(i - 1, j)
                if m: a_regroup(i + 1)
                if o: store(i - 1, 3)
                if f and not (isinstance(i, int) and i + 3 >= IMAGES): load(i + 3)
                if m: b_stacks(i + 1)

            load(0)
            sp.dma_start(wqkv_f, w_qkv.rearrange("(a p) n -> p a n", p=P)).then_inc(s_w, 16)
            sp.dma_start(wp_f, w_proj.rearrange("(a p) n -> p a n", p=P)).then_inc(s_w, 16)
            for n, w in enumerate((wq1, wq1, wk1, wk1)):
                sp.dma_start(wqk1_f[:, :, n * 32:(n + 1) * 32], w.rearrange("(a p) n -> p a n", p=P)).then_inc(s_w, 16)
            sp.dma_start(wv1_f, wv1.rearrange("(a p) n -> p a n", p=P)).then_inc(s_w, 16)
            sp.dma_start(bias[:], b_proj.rearrange("(o n) -> o n", o=1).broadcast_to([P, CH])).then_inc(s_const, 16)
            sp.dma_start(gam[:], gamma.rearrange("(o n) -> o n", o=1).broadcast_to([P, 1])).then_inc(s_const, 16)
            all_steps(sp, step)
            for j in range(4):
                sp.wait_ge(b_out[j], nth(IMAGES, 16, 0))

        @block.tensor
        def _(pe):
            def transposes(k, b, jobs):
                u = bufs[k]
                for j in jobs:
                    c, ct = divmod(j, CT)
                    if k == "a":
                        bank = j
                        pe.wait_ge(a_load[c], nth(b, 16, 16))
                        after(pe, a_ol, nth(b, 1, 0))
                    else:
                        bank = 2 + j % 2
                        pe.wait_ge(a_x1, nth(b, 4, 2 * (c + 1)))
                        if j < 2:
                            after(pe, b_vl, nth(b, 4, j - 1))
                        else:
                            pe.wait_ge(u["s_xt"], nth(b, 4, j - 1))
                    for t in range(TPC):
                        last = nc.tensor.transpose(u["ps"][:, bank, t * P:(t + 1) * P],
                                                   u["src"][:, c * TPC + t, ct * P:(ct + 1) * P], ident[:])
                    last.then_inc(u["s_tr"], 1)

            def group_mean(k, b):
                u = bufs[k]
                pe.wait_ge(u["s_mv"], nth(b, 2, 2))
                if k == "a":
                    after(pe, a_x1, nth(b, 4, -3))
                nc.tensor.matmul(u["ps"][:, u["bank"], 0:CT], group_avg[:], u["mv"][:, :, 0], start=True, stop=True).then_inc(u["s_gm"], 1)

            def group_var(k, b):
                u = bufs[k]
                pe.wait_ge(u["s_var"], nth(b, 1, 1))
                if k == "a":
                    after(pe, a_x1, nth(b, 4, -2))
                nc.tensor.matmul(u["ps"][:, u["bank"] + 1, 0:CT], group_avg[:], u["e"][:], start=True, stop=True).then_inc(u["s_gv"], 1)

            def project_T(out_ap, wh, wl, cols, c, nh, nl):
                tok = slice(c * CHUNK, (c + 1) * CHUNK)
                for ct in range(CT):
                    last = split3(out_ap, (wh[:, ct, cols], wl[:, ct, cols]), (nh[:, ct, tok], nl[:, ct, tok]),
                                  start=(ct == 0), stop=(ct == CT - 1))
                return last

            def project(out_ap, lhs, wh, wl, cols):
                for ct in range(CT):
                    last = split3(out_ap, (lhs[0][:, ct], lhs[1][:, ct]), (wh[:, ct, cols], wl[:, ct, cols]),
                                  start=(ct == 0), stop=(ct == CT - 1))
                return last

            def a_project_qk(b, c, ds):
                for d in ds:
                    pe.wait_ge(n_["a"]["nl"], nth(b, 4, 2 * c + 2))
                    if c:
                        pe.wait_ge(a_qke, nth(b, 8, d + 1))
                    else:
                        after(pe, a_x1, nth(b, 4, d - 3))
                    project_T(pa[:, d, :], wqkv_h, wqkv_l, slice(d * P, (d + 1) * P), c, a_nh, a_nl).then_inc(a_qk, 1)

            def a_project_v(b, js):
                for j in js:
                    pe.wait_ge(a_qke, nth(b, 8, 5 + j))
                    for t in range(2):
                        tok = slice((2 * j + t) * P, (2 * j + t + 1) * P)
                        last = project(pa[:, j, t * CH:(t + 1) * CH], (a_nh[:, :, tok], a_nl[:, :, tok]),
                                       wqkv_h, wqkv_l, slice(2 * CH, 3 * CH))
                    last.then_inc(a_v, 1)

            def a_scores(b, c):
                pe.wait_ge(a_qke, nth(b, 8, 8))
                pe.wait_ge(a_ve, nth(b, 4, 4))
                if c:
                    pe.wait_ge(a_sub, nth(b, 2, c))
                pe.nop(nofuse=True)
                for t in range(TPC):
                    for g in range(2):
                        for w in range(4):
                            n = (c * TPC + t) * 4 + w
                            tok = slice(n * WIN, (n + 1) * WIN)
                            for r in range(4):
                                rows = slice(32 * r, 32 * r + 32)
                                col = (2 * t + g) * WIN
                                last = nc.tensor.matmul(pa[32 * w:32 * w + 32, r, col:col + WIN],
                                                        qkT[rows, g, tok], qkT[rows, 2 + g, tok], start=True, stop=True)
                last.then_inc(a_s, 1)

            def a_output(b):
                pe.wait_ge(a_pt, nth(b, 2, 2))
                pe.nop(nofuse=True)
                for t in range(TILES):
                    for g in range(2):
                        for r in range(4):
                            h = 4 * g + r
                            blk = (r * 8 + 2 * (t % TPC) + g) * WIN
                            for w in range(4):
                                rows = slice(32 * w, 32 * w + 32)
                                col = (2 * t + g) * WIN
                                last = nc.tensor.matmul(pa[32 * r:32 * r + 32, w, col:col + WIN], v_tok[rows, t, h * DH:(h + 1) * DH],
                                                        pT[rows, t // TPC, blk:blk + WIN], start=True, stop=True)
                last.then_inc(a_o, 1)

            def a_projection(b, b_next):
                pe.wait_ge(a_ox, nth(b, 256, 256))
                for j in range(4):
                    if b_next:
                        pe.wait_ge(n_["a"]["xt"], nth(b, 4, 5 + j))
                    for t in range(2):
                        h = 2 * j + t
                        lhs = [o_dst[:, h % 4, :, part, h // 4, :] for part in (0, 1)]
                        last = project(pa[:, j, t * CH:(t + 1) * CH], lhs, wp_h, wp_l, slice(0, CH))
                    last.then_inc(a_y, 1)

            def b_project_qk(b):
                for c in range(CHUNKS):
                    pe.wait_ge(n_["b"]["nl"], nth(b, 4, 2 * c + 2))
                    project_T(pb[:, 2 + c, :], wqk1_h, wqk1_l, slice(0, P), c, b_nh, b_nl).then_inc(b_qk, 1)

            def b_project_v(b):
                for j in range(4):
                    if j < 2:
                        after(pe, b_y, nth(b, 8, j - 1))
                    else:
                        pe.wait_ge(b_vl, nth(b, 4, j - 1))
                    for t in range(2):
                        tok = slice((2 * j + t) * P, (2 * j + t + 1) * P)
                        last = project(pb[:, 2 + j % 2, t * CH:(t + 1) * CH], (b_nh[:, :, tok], b_nl[:, :, tok]), wv1_h, wv1_l, slice(0, CH))
                    last.then_inc(b_v, 1)

            def b_energy(b, it):
                pe.wait_ge(b_stack, nth(b, 64, 64))
                if it == 0:
                    after(pe, b_eh, nth(b, 8, 0))
                else:
                    pe.wait_ge(b_max, nth(b, 8, it))
                for c in range(CHUNKS):
                    last = nc.tensor.matmul(pb[:, c, :], k_stack[0:96, it * P:(it + 1) * P],
                                            q_stack[0:96, c * CHUNK:(c + 1) * CHUNK], start=True, stop=True)
                last.then_inc(b_s, 1)

            def b_max_rows(b):
                pe.wait_ge(b_dup, nth(b, 1, 1))
                for it in range(TILES):
                    last = nc.tensor.matmul(pb[96:98, it // TPC, (it % TPC) * P:(it % TPC + 1) * P],
                                            max_dup[:, it, :], ident[:], start=True, stop=True)
                last.then_inc(b_row, 1)

            def b_energy_T(b, jt):
                if jt == 0:
                    pe.wait_ge(b_rowl, nth(b, 1, 1))
                else:
                    pe.wait_ge(b_eh, nth(b, 8, jt))
                for c in range(CHUNKS):
                    last = nc.tensor.matmul(pb[:, c, :], q_stack[0:98, jt * P:(jt + 1) * P],
                                            k_stack[0:98, c * CHUNK:(c + 1) * CHUNK], start=True, stop=True)
                last.then_inc(b_st, 1)

            def b_output(b, it, b_next):
                pe.wait_ge(b_el, nth(b, 8, 8))
                if it >= 2:
                    pe.wait_ge(b_y, nth(b, 8, it - 1))
                elif b_next:
                    pe.wait_ge(b_qkl, nth(b, 2, 4))
                else:
                    pe.wait_ge(b_vl, nth(b, 4, 4))
                rows = slice(it * P, (it + 1) * P)
                for jt in range(TILES):
                    last = split3(pb[:, 2 + it % 2, 0:CH + 1], (e_h[:, jt, rows], e_l[:, jt, rows]),
                                  (v_h[:, jt, 0:CH + 1], v_l[:, jt, 0:CH + 1]), start=(jt == 0), stop=(jt == TILES - 1))
                last.then_inc(b_pv, 1)

            pe.wait_ge(s_const, 80)
            pe.wait_ge(s_wmax, 1)
            nc.tensor.transpose(pb[0:5, 0, 0:P], wmax[:], ident[:]).then_inc(s_wmaxT, 1)
            pe.wait_ge(s_diag, 1)
            nc.tensor.matmul(pb[:, 1, 0:5], ones5[:], wmax_diag[:], start=True, stop=True).then_inc(s_unit_ps, 1)
            pe.wait_ge(s_ready, 1)

            def step(i, b, o, m, f):
                for it in range(TILES):
                    if b: b_energy(i, it)
                    if o: b_output(i - 1, it, b)
                    if m and it == 0: a_scores(i + 1, 1)
                    if m and it == 4: a_output(i + 1)
                if f: transposes("a", i + 2, range(4))
                if b: b_max_rows(i)
                if b: b_project_v(i)
                if m: a_projection(i + 1, f)
                if b: b_energy_T(i, 0)
                if m: transposes("b", i + 1, range(4))
                if f: group_mean("a", i + 2)
                if b: b_energy_T(i, 1)
                if f: group_var("a", i + 2)
                if b: b_energy_T(i, 2)
                if m: group_mean("b", i + 1)
                if f: a_project_qk(i + 2, 0, range(0, 2))
                if m: group_var("b", i + 1)
                if b: b_energy_T(i, 3)
                if f: a_project_qk(i + 2, 0, range(2, 4))
                if b: b_energy_T(i, 4)
                if f: a_project_qk(i + 2, 1, range(0, 2))
                if b: b_energy_T(i, 5)
                if f: a_project_qk(i + 2, 1, range(2, 4))
                if b: b_energy_T(i, 6)
                if m: b_project_qk(i + 1)
                if f: a_project_v(i + 2, range(0, 2))
                if b: b_energy_T(i, 7)
                if f: a_project_v(i + 2, range(2, 4))
                if f: a_scores(i + 2, 0)

            all_steps(pe, step)

        @block.scalar
        def _(act):
            def copy_T(k, b):
                u = bufs[k]
                for c in range(CHUNKS):
                    for ct in range(CT):
                        j = c * CT + ct
                        act.wait_ge(u["s_tr"], nth(b, 4, j + 1))
                        nc.scalar.activation(u["xT"][:, ct, c * CHUNK:(c + 1) * CHUNK], u["ps"][:, j if k == "a" else 2 + j % 2, :], ACT.Copy).then_inc(u["s_xt"], 1)

            def normalise(k, b, last):
                u = bufs[k]
                act.wait_ge(u["s_nb"], nth(b, 1, 1))
                for c in range(CHUNKS):
                    for ct in range(CT):
                        j = c * CT + ct
                        if last is not None:
                            act.wait_ge(n_[last[0]]["nl"], nth(last[1], 4, j + 1))
                        if k == "a":
                            src = u["xT"][:, ct, :].rearrange("p (w t k) -> p t w k", w=4, k=WIN)[:, c * TPC:(c + 1) * TPC]
                            dst = u["xn"][:, j, :].rearrange("p (t w k) -> p t w k", w=4, k=WIN)
                        else:
                            src, dst = u["xT"][:, ct, c * CHUNK:(c + 1) * CHUNK], u["xn"][:, j, :]
                        nc.scalar.activation(dst, src, ACT.Identity,
                                             scale=u["r"][:, ct:ct + 1], bias=u["nb"][:, ct:ct + 1]).then_inc(u["s_xn"], 1)

            def a_copy_qk(b, c, ds):
                for d in ds:
                    act.wait_ge(a_qk, nth(b, 8, 4 * c + d + 1))
                    dst = qkT[:, d, c * CHUNK:(c + 1) * CHUNK]
                    after(act, a_s, nth(b, 2, 0))
                    if d < 2:
                        for u in range(2):
                            last = nc.scalar.activation(dst.rearrange("p (n s u i) -> p u n s i", s=4, u=2, i=4)[:, u],
                                                        pa[:, d, :].rearrange("p (n i u s) -> p u n s i", s=4, u=2, i=4)[:, u],
                                                        ACT.Copy, scale=f_q[:, 0:1])
                        last.then_inc(a_qke, 1)
                    else:
                        nc.scalar.activation(dst, pa[:, d, :], ACT.Copy).then_inc(a_qke, 1)

            def a_copy_v(b, js):
                for j in js:
                    act.wait_ge(a_v, nth(b, 4, j + 1))
                    after(act, a_o, nth(b, 1, 0))
                    nc.scalar.activation(v_tok[:, 2 * j:2 * j + 2, :].rearrange("p t n -> p (t n)"), pa[:, j, :], ACT.Copy).then_inc(a_ve, 1)

            def a_exponential(b, c):
                act.wait_ge(a_sub, nth(b, 2, c + 1))
                nc.scalar.activation(s32[:, c, :], s32[:, c, :], ACT.Exp).then_inc(a_exp, 1)

            def a_out_high(b):
                act.wait_ge(a_o, nth(b, 1, 1))
                after(act, a_ox, nth(b, 256, 0))
                for g in range(2):
                    last = nc.scalar.activation(out_parts(0, g), out_banks(g), ACT.Copy)
                last.then_inc(a_oh, 1)

            def b_qk_high(b):
                for c in range(CHUNKS):
                    act.wait_ge(b_qk, nth(b, 2, c + 1))
                    nc.scalar.activation(qk_h[:, c * CHUNK:(c + 1) * CHUNK], pb[:, 2 + c, :], ACT.Copy).then_inc(b_qkh, 1)

            def b_v_high(b):
                for j in range(4):
                    act.wait_ge(b_v, nth(b, 4, j + 1))
                    after(act, b_pv, nth(b, 8, 0))
                    nc.scalar.activation(v_h[:, 2 * j:2 * j + 2, 0:CH], pb[:, 2 + j % 2, :].rearrange("p (t n) -> p t n", t=2), ACT.Copy).then_inc(b_vh, 1)

            def b_row_high(b):
                act.wait_ge(b_row, nth(b, 1, 1))
                nc.scalar.activation(max_row[96:98, :], pb[96:98, 0:2, :].rearrange("p a n -> p (a n)"), ACT.Copy).then_inc(b_rowh, 1)

            def b_exponential(b, jt):
                act.wait_ge(b_st, nth(b, 8, jt + 1))
                after(act, b_el, nth(b, 8, jt - 1))
                src = pb[:, 0:2, :].rearrange("p a n -> p (a n)")
                nc.scalar.activation(e32[:, jt % 2, :], src, ACT.Exp, scale=f_energy[:, 0:1]).then_inc(b_exp, 1)
                nc.scalar.activation(e_h[:, jt, :], src, ACT.Exp, scale=f_energy[:, 0:1]).then_inc(b_eh, 1)

            act.wait_ge(s_ready, 1)

            def step(i, b, o, m, f):
                if m: a_exponential(i + 1, 0)
                if m: a_exponential(i + 1, 1)
                if m: a_out_high(i + 1)
                if f: copy_T("a", i + 2)
                if b: b_row_high(i)
                if b: b_v_high(i)
                if b: b_exponential(i, 0)
                if m: copy_T("b", i + 1)
                if b: b_exponential(i, 1)
                if f: normalise("a", i + 2, ("b", i) if b else ("a", i + 1) if m else None)
                if b: b_exponential(i, 2)
                if f: a_copy_qk(i + 2, 0, range(0, 2))
                if b: b_exponential(i, 3)
                if m: normalise("b", i + 1, ("a", i + 2) if f else ("b", i))
                if f: a_copy_qk(i + 2, 0, range(2, 4))
                if b: b_exponential(i, 4)
                if f: a_copy_qk(i + 2, 1, range(0, 2))
                if b: b_exponential(i, 5)
                if f: a_copy_qk(i + 2, 1, range(2, 4))
                if b: b_exponential(i, 6)
                if m: b_qk_high(i + 1)
                if f: a_copy_v(i + 2, range(0, 2))
                if b: b_exponential(i, 7)
                if f: a_copy_v(i + 2, range(2, 4))

            all_steps(act, step)

        @block.vector
        def _(dve):
            def stats(k, b):
                u = bufs[k]
                for c in range(CHUNKS):
                    for ct in range(CT):
                        dve.wait_ge(u["s_xt"], nth(b, 4, c * CT + ct + 1))
                        nc.vector.bn_stats(u["st"][:, ct, c, :], u["xT"][:, ct, c * CHUNK:(c + 1) * CHUNK]).then_inc(u["s_bn"], 1)
                dve.wait_ge(u["s_bn"], nth(b, 4, 4))
                dve.nop(nofuse=True)
                for ct in range(CT):
                    nc.vector.bn_aggr(u["mv"][:, ct, :], u["st"][:, ct].rearrange("p c s -> p (c s)")).then_inc(u["s_mv"], 1)

            def group_mean(k, b):
                u = bufs[k]
                dve.wait_ge(u["s_gm"], nth(b, 1, 1))
                nc.vector.tensor_scalar(u["gm"][:], u["ps"][:, u["bank"], 0:CT], -1.0, None, ALU.mult).then_inc(u["s_gmc"], 1)
                dve.wait_ge(u["s_gmc"], nth(b, 1, 1))
                nc.vector.tensor_tensor(u["d"][:], u["mv"][:, :, 0], u["gm"][:], ALU.add).then_inc(u["s_dev"], 1)
                dve.wait_ge(u["s_dev"], nth(b, 1, 1))
                nc.vector.tensor_tensor(u["e"][:], u["d"][:], u["d"][:], ALU.mult).then_inc(u["s_sq"], 1)
                dve.wait_ge(u["s_sq"], nth(b, 1, 1))
                nc.vector.tensor_tensor(u["e"][:], u["e"][:], u["mv"][:, :, 1], ALU.add).then_inc(u["s_var"], 1)

            def group_scale(k, b):
                u = bufs[k]
                dve.wait_ge(u["s_gv"], nth(b, 1, 1))
                nc.vector.tensor_scalar(u["ve"][:], u["ps"][:, u["bank"] + 1, 0:CT], EPS, None, ALU.add).then_inc(u["s_ve"], 1)

            def norm_high(k, b):
                u = bufs[k]
                for c in range(CHUNKS):
                    for ct in range(CT):
                        j = c * CT + ct
                        dve.wait_ge(u["s_xn"], nth(b, 4, j + 1))
                        after(dve, a_v if k == "a" else b_v, nth(b, 4, 0))
                        nc.vector.tensor_copy(u["nh"][:, ct, c * CHUNK:(c + 1) * CHUNK], u["xn"][:, j, :]).then_inc(u["s_nh"], 1)

            heads4 = dict(n=8, k=WIN)

            def a_maximum(b, c):
                dve.wait_ge(a_s, nth(b, 2, c + 1))
                s = pa[:, :, 0:CH].rearrange("p r (n k) -> p r n k", **heads4)
                m = a_rmax[:, c, :].rearrange("p (r n) -> p r n", r=4)
                nc.vector.tensor_reduce(m, s, X, ALU.max).then_inc(a_max, 1)
                dve.wait_ge(a_max, nth(b, 2, c + 1))
                nc.vector.tensor_tensor(s32[:, c, :].rearrange("p (r n k) -> p r n k", r=4, k=WIN), s,
                                        m.unsqueeze(3).broadcast_to([P, 4, 8, WIN]), ALU.subtract).then_inc(a_sub, 1)

            def a_row_sum(b, c):
                dve.wait_ge(a_exp, nth(b, 2, c + 1))
                nc.vector.tensor_reduce(a_rsum[:, c, :], s32[:, c, :].rearrange("p (n k) -> p n k", k=WIN), X, ALU.add).then_inc(a_sum, 1)
                dve.wait_ge(a_sum, nth(b, 2, c + 1))
                nc.vector.reciprocal(a_rinv[:, c, :], a_rsum[:, c, :]).then_inc(a_inv, 1)

            def a_transpose(b, c):
                dve.wait_ge(a_prob, nth(b, 2, c + 1))
                after(dve, a_o, nth(b, 1, 0))
                nc.vector.transpose(pT[:, c, :], s32[:, c, :]).then_inc(a_pt, 1)

            def a_out_low(b):
                dve.wait_ge(a_oh, nth(b, 1, 1))
                for g in range(2):
                    last = nc.vector.tensor_tensor(out_parts(1, g), out_banks(g), out_parts(0, g), ALU.subtract)
                last.then_inc(a_ol, 1)

            def a_residual(b):
                dve.wait_ge(a_xb, nth(b, 1, 1))
                after(dve, n_["b"]["tr"], nth(b, 4, 0))
                for j in range(4):
                    after(dve, b_copy, nth(b, 4, j - 3))
                    dve.wait_ge(a_y, nth(b, 4, j + 1))
                    nc.vector.scalar_tensor_tensor(x1[:, 2 * j:2 * j + 2, :].rearrange("p t n -> p (t n)"), pa[:, j, :], f_proj[:, 0:1],
                                                   xb[:, 2 * j:2 * j + 2, :].rearrange("p t n -> p (t n)"), ALU.mult, ALU.add).then_inc(a_x1, 1)

            def b_qk_low(b):
                after(dve, b_stack, nth(b, 64, 0))
                for c in range(CHUNKS):
                    dve.wait_ge(b_qkh, nth(b, 2, c + 1))
                    cols = slice(c * CHUNK, (c + 1) * CHUNK)
                    nc.vector.scalar_tensor_tensor(qk_hl[:, cols], qk_h[:, cols], masks[:, 0:1], pb[:, 2 + c, :],
                                                   ALU.mult, ALU.add).then_inc(b_qkl, 1)

            def b_v_low(b):
                for j in range(4):
                    dve.wait_ge(b_vh, nth(b, 4, j + 1))
                    nc.vector.tensor_tensor(v_l[:, 2 * j:2 * j + 2, 0:CH], pb[:, 2 + j % 2, :].rearrange("p (t n) -> p t n", t=2),
                                            v_h[:, 2 * j:2 * j + 2, 0:CH], ALU.subtract).then_inc(b_vl, 1)

            def b_maximum(b, it):
                dve.wait_ge(b_s, nth(b, 8, it + 1))
                nc.vector.tensor_reduce(max_neg[:, it:it + 1], pb[:, 0:2, :].rearrange("p a n -> p (a n)"),
                                        X, ALU.max, negate=True).then_inc(b_max, 1)

            def b_duplicate(b):
                dve.wait_ge(b_max, nth(b, 8, 8))
                nc.vector.tensor_scalar(max_dup[:], max_neg[:].unsqueeze(2).broadcast_to([P, TILES, 2]),
                                        1.0 / ROW_SCALE, None, ALU.mult).then_inc(b_dup, 1)

            def b_row_low(b):
                dve.wait_ge(b_rowh, nth(b, 1, 1))
                nc.vector.scalar_tensor_tensor(k_stack[96:98, :], max_row[96:98, :], masks[96:98, 1:2],
                                               pb[96:98, 0:2, :].rearrange("p a n -> p (a n)"), ALU.mult, ALU.add).then_inc(b_rowl, 1)

            def b_exp_low(b, jt):
                dve.wait_ge(b_eh, nth(b, 8, jt + 1))
                nc.vector.tensor_tensor(e_l[:, jt, :], e32[:, jt % 2, :], e_h[:, jt, :], ALU.subtract).then_inc(b_el, 1)

            def b_result(b, it):
                dve.wait_ge(b_copy, nth(b, 4, it // 2 + 1))
                dve.wait_ge(b_pv, nth(b, 8, it + 1))
                nc.vector.reciprocal(y_inv[:, it:it + 1], pb[:, 2 + it % 2, CH:CH + 1]).then_inc(b_yinv, 1)
                dve.wait_ge(b_yinv, nth(b, 8, it + 1))
                nc.vector.tensor_tensor(y_fac[:, it:it + 1], y_inv[:, it:it + 1], f_out[:, 0:1], ALU.mult).then_inc(b_yfac, 1)
                dve.wait_ge(b_yfac, nth(b, 8, it + 1))
                nc.vector.scalar_tensor_tensor(y[:, it, :], pb[:, 2 + it % 2, 0:CH], y_fac[:, it:it + 1], y[:, it, :],
                                               ALU.mult, ALU.add).then_inc(b_y, 1)

            def step(i, b, o, m, f):
                if m: a_maximum(i + 1, 0)
                if b: b_maximum(i, 0)
                if o: b_result(i - 1, 0)
                if m: a_row_sum(i + 1, 0)
                if m: a_maximum(i + 1, 1)
                if b: b_maximum(i, 1)
                if o: b_result(i - 1, 1)
                if b: b_maximum(i, 2)
                if m: a_row_sum(i + 1, 1)
                if m: a_transpose(i + 1, 0)
                if o: b_result(i - 1, 2)
                if b: b_maximum(i, 3)
                if m: a_transpose(i + 1, 1)
                if o: b_result(i - 1, 3)
                if b: b_maximum(i, 4)
                if o: b_result(i - 1, 4)
                if b: b_maximum(i, 5)
                if m: a_out_low(i + 1)
                if o: b_result(i - 1, 5)
                if b: b_maximum(i, 6)
                if o: b_result(i - 1, 6)
                if b: b_maximum(i, 7)
                if b: b_duplicate(i)
                if o: b_result(i - 1, 7)
                if f: stats("a", i + 2)
                if b: b_row_low(i)
                if b: b_v_low(i)
                if m: a_residual(i + 1)
                if f: group_mean("a", i + 2)
                if b: b_exp_low(i, 0)
                if f: group_scale("a", i + 2)
                if m: stats("b", i + 1)
                if b: b_exp_low(i, 1)
                if f: norm_high("a", i + 2)
                if m: group_mean("b", i + 1)
                if b: b_exp_low(i, 2)
                if m: group_scale("b", i + 1)
                if b: b_exp_low(i, 3)
                if m: norm_high("b", i + 1)
                if b: b_exp_low(i, 4)
                if b: b_exp_low(i, 5)
                if b: b_exp_low(i, 6)
                if m: b_qk_low(i + 1)
                if b: b_exp_low(i, 7)

            chain = [0]

            def link(ins):
                chain[0] += 1
                ins.then_inc(s_chain, 1)
                dve.wait_ge(s_chain, chain[0])

            dve.wait_ge(s_const, 80)
            dve.wait_ge(s_w, 112)
            for n, w in enumerate((wqkv_f, wp_f, wqk1_f[:, :, 0:32], wqk1_f[:, :, 64:96], wv1_f)):
                last = nc.vector.tensor_reduce(wmax[:, n:n + 1], w, mybir.AxisListType.XY, ALU.max, apply_absolute_value=True)
            last.then_inc(s_wmax, 1)
            dve.wait_ge(s_wmaxT, 1)
            link(nc.vector.tensor_reduce(wmax_all[:], pb[0:5, 0, 0:P], X, ALU.max))
            link(nc.vector.tensor_scalar(wmax_all[:], wmax_all[:], 1e-30, 2.0, ALU.max, ALU.mult))
            link(nc.vector.memset(ones5[:], 1.0))
            nc.vector.tensor_scalar(wmax_diag[:], ident[0:5, 0:5], wmax_all[:, 0:1], None, ALU.mult).then_inc(s_diag, 1)
            dve.wait_ge(s_unit_ps, 1)
            link(nc.vector.tensor_copy(unit[:], pb[:, 1, 0:5]))
            link(nc.vector.reciprocal(unit_inv[:], unit[:]))
            link(nc.vector.scalar_tensor_tensor(f_q[:], unit[:, 0:1], DH ** -0.5, unit[:, 0:1], ALU.mult, ALU.mult))
            link(nc.vector.tensor_tensor(f_proj[:], unit[:, 0:1], unit[:, 1:2], ALU.mult))
            link(nc.vector.tensor_tensor(f_energy[:], unit[:, 2:3], unit[:, 3:4], ALU.mult))
            link(nc.vector.tensor_tensor(f_out[:], unit[:, 4:5], gam[:], ALU.mult))
            for w, n in ((wqkv_f, 0), (wp_f, 1), (wqk1_f[:, :, 0:64], 2), (wqk1_f[:, :, 64:128], 3), (wv1_f, 4)):
                link(nc.vector.tensor_scalar(w, w, unit_inv[:, n:n + 1], None, ALU.mult))
            for f, h, l in weights:
                link(nc.vector.tensor_copy(h[:], f))
            for f, h, l in weights:
                last = nc.vector.tensor_tensor(l[:], f, h[:], ALU.subtract)
            dve.wait_ge(s_pool, 5)
            last.then_inc(s_ready, 1)
            all_steps(dve, step)

        @block.gpsimd
        def _(pool):
            def rstd(k, b):
                u = bufs[k]
                pool.wait_ge(u["s_ve"], nth(b, 1, 1))
                nc.gpsimd.tensor_tensor(u["r"][:], u["ve"][:], minus_half[:], ALU.pow).then_inc(u["s_r"], 1)
                pool.wait_ge(u["s_r"], nth(b, 1, 1))
                nc.gpsimd.tensor_tensor(u["nb"][:], u["gm"][:], u["r"][:], ALU.mult).then_inc(u["s_nb"], 1)

            def norm_low(k, b):
                u = bufs[k]
                for c in range(CHUNKS):
                    for ct in range(CT):
                        j = c * CT + ct
                        cols = slice(c * CHUNK, (c + 1) * CHUNK)
                        pool.wait_ge(u["s_nh"], nth(b, 4, j + 1))
                        nc.gpsimd.tensor_tensor(u["nl"][:, ct, cols], u["xn"][:, j, :], u["nh"][:, ct, cols], ALU.subtract).then_inc(u["s_nl"], 1)

            def add_bias(b):
                for c in range(CHUNKS):
                    pool.wait_ge(a_load[c], nth(b, 16, 16))
                after(pool, a_x1, nth(b, 4, 0))
                nc.gpsimd.tensor_tensor(xb[:], xin[:], bias[:].unsqueeze(1).broadcast_to([P, TILES, CH]), ALU.add).then_inc(a_xb, 1)

            def a_probabilities(b, c):
                pool.wait_ge(a_inv, nth(b, 2, c + 1))
                v = s32[:, c, :].rearrange("p (n k) -> p n k", k=WIN)
                nc.gpsimd.tensor_tensor(v, v, a_rinv[:, c, :].unsqueeze(2).broadcast_to([P, 32, WIN]), ALU.mult).then_inc(a_prob, 1)

            def b_keep(b, j):
                pool.wait_ge(a_x1, nth(b, 4, j + 1))
                after(pool, b_out[j], nth(b, 16, 0))
                pool.nop(nofuse=True)
                nc.gpsimd.tensor_copy(y[:, 2 * j:2 * j + 2, :], x1[:, 2 * j:2 * j + 2, :]).then_inc(b_copy, 1)

            def step(i, b, o, m, f):
                if m: a_probabilities(i + 1, 0)
                if m: a_probabilities(i + 1, 1)
                for j in range(4):
                    if b: b_keep(i, j)
                if f: rstd("a", i + 2)
                if f: norm_low("a", i + 2)
                if m: rstd("b", i + 1)
                if m: norm_low("b", i + 1)
                if f: add_bias(i + 2)

            nc.gpsimd.memset(q_stack[96:128, :], ROW_SCALE).then_inc(s_pool, 1)
            pool.wait_ge(s_pool, 1)
            nc.gpsimd.memset(k_stack[96:128, :], 0.0).then_inc(s_pool, 1)
            pool.wait_ge(s_pool, 2)
            nc.gpsimd.memset(v_h[:, :, CH:VCOL], 1.0).then_inc(s_pool, 1)
            nc.gpsimd.memset(v_l[:, :, CH:VCOL], 0.0).then_inc(s_pool, 1)
            nc.gpsimd.memset(minus_half[:], -0.5).then_inc(s_pool, 1)
            pool.wait_ge(s_pool, 5)
            pool.wait_ge(s_const, 80)
            all_steps(pool, step)


_INS = ["x", "L0_conv_w_qkv", "L0_conv_w_proj", "L0_conv_b_proj", "L1_conv_Wq", "L1_conv_Wk", "L1_conv_Wv", "L1_conv_gamma"]


def kernel(**inputs):
    import numpy as _np
    import concourse.bacc as _bacc
    from concourse import mybir as _mybir
    from concourse.bass_utils import run_bass_kernel_spmd as _run

    nc = _bacc.Bacc("TRN2", target_bir_lowering=False, num_devices=1)
    arrays = {f"in_{name}": _np.ascontiguousarray(inputs[name]) for name in _INS}
    n = _np.arange(P)
    arrays["in_ident"] = _np.eye(P, dtype=_np.float32)
    arrays["in_group"] = _np.kron(_np.eye(P // GROUP), _np.full((GROUP, GROUP), 1.0 / GROUP)).astype(_np.float32)
    masks = _np.zeros((P, 2), _np.float32)
    masks[32:64, 0] = masks[96:128, 0] = -1.0
    masks[97, 1] = -1.0
    arrays["in_masks"] = masks
    args = [nc.dram_tensor(name, a.shape, _mybir.dt.from_np(a.dtype), kind="ExternalInput").ap() for name, a in arrays.items()]
    out = nc.dram_tensor("out_0", (IMAGES, 32, 32, CH), _mybir.dt.float32, kind="ExternalOutput").ap()
    build(nc, *args, out)
    r = _run(nc, [arrays], core_ids=[0])
    return r.results[0]["out_0"]
```

```python
import concourse.bass as bass
from concourse import mybir
from contextlib import ExitStack

F32 = mybir.dt.float32
F16 = mybir.dt.float16
ALU = mybir.AluOpType
ACT = mybir.ActivationFunctionType
X = mybir.AxisListType.X

P = 128
IMAGES, TOKENS, CH = 8, 1024, 256
TILES = TOKENS // P
CT = CH // P
CHUNK = 512
CHUNKS = TOKENS // CHUNK
TPC = CHUNK // P
HEADS, DH = 8, 32
WIN = 32
GROUP = 8
VCOL = CH + 2
EPS = 1e-5
ROW_SCALE = 2.0 ** 15


def nth(b, per, n):
    return b * per + n


def build(nc, x, w_qkv, w_proj, b_proj, wq1, wk1, wv1, gamma, ident_d, group_d, masks_d, out):
    x_v = x.rearrange("b (t y) w c -> b t (y w) c", t=TILES)
    out_v = out.rearrange("b (t y) w c -> b t (y w) c", t=TILES)

    with ExitStack() as ctx:
        def sb(name, shape, dt=F32):
            return ctx.enter_context(nc.sbuf_tensor(name, shape, dt))

        def sem(name):
            return ctx.enter_context(nc.semaphore(name))

        ident = sb("ident", [P, P])
        group_avg = sb("group_avg", [P, P])
        masks = sb("masks", [P, 2])
        bias = sb("bias", [P, CH])
        gam = sb("gam", [P, 1])
        wqkv_h, wqkv_l = sb("wqkv_h", [P, CT, 3 * CH], F16), sb("wqkv_l", [P, CT, 3 * CH], F16)
        wp_h, wp_l = sb("wp_h", [P, CT, CH], F16), sb("wp_l", [P, CT, CH], F16)
        wqk1_h, wqk1_l = sb("wqk1_h", [P, CT, P], F16), sb("wqk1_l", [P, CT, P], F16)
        wv1_h, wv1_l = sb("wv1_h", [P, CT, CH], F16), sb("wv1_l", [P, CT, CH], F16)
        wmax = sb("wmax", [P, 5])
        wmax_all = sb("wmax_all", [5, 1])
        wmax_diag = sb("wmax_diag", [5, 5])
        ones5 = sb("ones5", [5, P])
        unit = sb("unit", [P, 5])
        unit_inv = sb("unit_inv", [P, 5])
        f_q = sb("f_q", [P, 1])
        f_proj = sb("f_proj", [P, 1])
        f_energy = sb("f_energy", [P, 1])
        f_out = sb("f_out", [P, 1])
        minus_half = sb("minus_half", [P, CT])
        xin = sb("xin", [P, TILES, CH])
        xb = sb("xb", [P, TILES, CH])
        x1 = sb("x1", [P, TILES, CH])
        a_xT = sb("a_xT", [P, CT, TOKENS])
        xn32 = sb("xn32", [P, CHUNKS * CT, CHUNK])
        a_nh, a_nl = sb("a_nh", [P, CT, TOKENS], F16), sb("a_nl", [P, CT, TOKENS], F16)
        qkT = sb("qkT", [P, 4, TOKENS])
        v_tok = sb("v_tok", [P, TILES, CH])
        s32 = sb("s32", [P, CHUNKS, TPC * CH])
        pT = sb("pT", [P, CHUNKS, TPC * CH])
        o_src = sb("o_src", [P, 4, 2, 2, 2, P], F16)
        o_dst = sb("o_dst", [P, 4, 2, 2, 2, P], F16)
        a_rmax, a_rsum = sb("a_rmax", [P, CHUNKS, 32]), sb("a_rsum", [P, CHUNKS, 32])
        a_rinv = sb("a_rinv", [P, CHUNKS, 32])
        y = sb("y", [P, TILES, CH])
        b_nh, b_nl = sb("b_nh", [P, CT, TOKENS], F16), sb("b_nl", [P, CT, TOKENS], F16)
        b_xT = sb("b_xT", [P, CT, TOKENS])
        qk_h = sb("qk_h", [P, TOKENS], F16)
        qk_hl = sb("qk_hl", [P, TOKENS], F16)
        q_stack = sb("q_stack", [P, TOKENS], F16)
        k_stack = sb("k_stack", [P, TOKENS], F16)
        v_h, v_l = sb("v_h", [P, TILES, VCOL], F16), sb("v_l", [P, TILES, VCOL], F16)
        max_neg = sb("max_neg", [P, TILES])
        max_dup = sb("max_dup", [P, TILES, 2])
        max_row = qk_h
        e32 = sb("e32", [P, 2, TOKENS])
        e_h, e_l = sb("e_h", [P, TILES, TOKENS], F16), sb("e_l", [P, TILES, TOKENS], F16)
        y_inv = sb("y_inv", [P, TILES])
        y_fac = sb("y_fac", [P, TILES])
        norm = {k: dict(st=sb(k + "st", [P, CT, CHUNKS, 6]), mv=sb(k + "mv", [P, CT, 2]),
                        gm=sb(k + "gm", [P, CT]), d=sb(k + "d", [P, CT]), e=sb(k + "e", [P, CT]),
                        ve=sb(k + "ve", [P, CT]), r=sb(k + "r", [P, CT]), nb=sb(k + "nb", [P, CT])) for k in "ab"}
        stage = e_l[:].rearrange("p t n -> p (t n)").bitcast(F32)
        wqkv_f = stage[:, 0:1536].rearrange("p (a n) -> p a n", a=CT)
        wp_f = stage[:, 1536:2048].rearrange("p (a n) -> p a n", a=CT)
        wqk1_f = stage[:, 2048:2304].rearrange("p (a n) -> p a n", a=CT)
        wv1_f = stage[:, 2304:2816].rearrange("p (a n) -> p a n", a=CT)
        scaled = [(wqkv_f, wqkv_h[:], wqkv_l[:], 0), (wp_f, wp_h[:], wp_l[:], 1),
                  (wqk1_f[:, :, 0:64], wqk1_h[:, :, 0:64], wqk1_l[:, :, 0:64], 2),
                  (wqk1_f[:, :, 64:128], wqk1_h[:, :, 64:128], wqk1_l[:, :, 64:128], 3), (wv1_f, wv1_h[:], wv1_l[:], 4)]

        pa = ctx.enter_context(nc.psum_tensor("pa", [P, 4, CHUNK], F32))
        pb = ctx.enter_context(nc.psum_tensor("pb", [P, 4, CHUNK], F32))

        s_const, s_chain = sem("s_const"), sem("s_chain")
        s_wqkv, s_wp, s_wqk1, s_wv1 = sem("s_wqkv"), sem("s_wp"), sem("s_wqk1"), sem("s_wv1")
        s_wmax, s_wmaxT, s_diag, s_unit_ps, s_ready = sem("s_wmax"), sem("s_wmaxT"), sem("s_diag"), sem("s_unit_ps"), sem("s_ready")
        s_unit, s_high = sem("s_unit"), sem("s_high")
        s_pool = sem("s_pool")
        a_load = [sem(f"a_load{c}") for c in range(CHUNKS)]
        a_xb = sem("a_xb")
        a_x1 = sem("a_x1")
        a_s = sem("a_s")
        a_o = sem("a_o")
        a_y = sem("a_y")
        a_qk = sem("a_qk")
        a_v = sem("a_v")
        a_qe = sem("a_qe")
        a_ke = sem("a_ke")
        a_ve = sem("a_ve")
        a_max = sem("a_max")
        a_sub = sem("a_sub")
        a_exp = sem("a_exp")
        a_sum = sem("a_sum")
        a_inv = sem("a_inv")
        a_prob = sem("a_prob")
        a_pt = sem("a_pt")
        a_oh = sem("a_oh")
        a_ol = sem("a_ol")
        a_ox = sem("a_ox")
        b_copy = sem("b_copy")
        b_qk = sem("b_qk")
        b_qkh = sem("b_qkh")
        b_qkl = sem("b_qkl")
        b_stack = sem("b_stack")
        b_v = sem("b_v")
        b_vh = sem("b_vh")
        b_vl = sem("b_vl")
        b_s = sem("b_s")
        b_max = sem("b_max")
        b_dup = sem("b_dup")
        b_row = sem("b_row")
        b_rowh = sem("b_rowh")
        b_rowl = sem("b_rowl")
        b_st = sem("b_st")
        b_exp = sem("b_exp")
        b_eh = sem("b_eh")
        b_el = sem("b_el")
        b_pv = sem("b_pv")
        b_yinv = sem("b_yinv")
        b_yfac = sem("b_yfac")
        b_y = sem("b_y")
        b_out = [sem(f"b_out{j}") for j in range(4)]
        n_ = {k: {e: sem(f"{k}n_{e}") for e in (
            "tr",
            "xt",
            "bn",
            "mv",
            "gm",
            "gmc",
            "dev",
            "sq",
            "var",
            "gv",
            "ve",
            "r",
            "nb",
            "xn",
            "nh",
            "nl",
        )} for k in "ab"}
        bufs = {"a": dict(src=xin, xT=a_xT, xn=xn32, nh=a_nh, nl=a_nl, ps=pa, col=384, **norm["a"], **{"s_" + k: v for k, v in n_["a"].items()}),
                "b": dict(src=x1, xT=b_xT, xn=xn32, nh=b_nh, nl=b_nl, ps=pb, col=0, **norm["b"], **{"s_" + k: v for k, v in n_["b"].items()})}

        def after(eng, s, value):
            if not (isinstance(value, int) and value <= 0):
                eng.wait_ge(s, value)

        def all_steps(eng, first, second):
            def peeled(half, i):
                half(i, *(0 <= n < IMAGES for n in (i, i - 1, i + 1, i + 2)))
            for i in range(-1, 2):
                peeled(first, i)
                peeled(second, i)
            with eng.Fori(2, IMAGES - 3) as i:
                first(i, True, True, True, True)
                second(i, True, True, True, True)
            for i in range(IMAGES - 3, IMAGES + 1):
                peeled(first, i)
                peeled(second, i)

        def split3(out_ap, lhs, rhs, start=True, stop=True):
            (lh, ll), (rh, rl) = lhs, rhs
            nc.tensor.matmul(out_ap, lh, rh, start=start, stop=False)
            nc.tensor.matmul(out_ap, lh, rl, start=False, stop=False)
            return nc.tensor.matmul(out_ap, ll, rh, start=False, stop=stop)

        def last_image(b):
            return isinstance(b, int) and b == IMAGES - 1

        def result_bank(b, it):
            if last_image(b):
                it = it % 6
                return pa[:, it, :] if it < 4 else pb[:, it - 2, :]
            return pb[:, 2 + it % 2, :]

        def out_banks(g):
            return pa[:].rearrange("p w (t g su i) -> p g (w t) su i", t=TILES, g=2, i=4)[:, g]

        def out_parts(part, g):
            return o_src[:].rearrange("p s u l g (n i) -> p l g n (s u) i", i=4)[:, part, g]

        def store_pair(eng, b, j):
            dst = out_v[b] if isinstance(b, int) else out_v[bass.ds(b, 1)].rearrange("o t p c -> (o t) p c")
            eng.wait_ge(b_y, nth(b, 8, 2 * j + 2))
            eng.nop(nofuse=True)
            eng.dma_start(dst[2 * j:2 * j + 2].rearrange("t p c -> p t c"), y[:, 2 * j:2 * j + 2, :]).then_inc(b_out[j], 16)

        block = ctx.enter_context(nc.Block())

        @block.sync
        def _(sp):
            sp.dma_start(ident[:], ident_d).then_inc(s_const, 16)

            def load(b):
                for c in range(CHUNKS):
                    after(sp, n_["a"]["tr"], nth(b, 4, 0))
                    sp.nop(nofuse=True)
                    after(sp, a_xb, nth(b, 1, 0))
                    sp.nop(nofuse=True)
                    src = x_v[b] if isinstance(b, int) else x_v[bass.ds(b, 1)].rearrange("o t p c -> (o t) p c")
                    sp.dma_start(xin[:, c * TPC:(c + 1) * TPC, :],
                                 src[c * TPC:(c + 1) * TPC].rearrange("t p c -> p t c")).then_inc(a_load[c], 16)

            def b_stacks(b):
                sp.wait_ge(b_qkl, nth(b, 2, 2))
                sp.nop(nofuse=True)
                after(sp, b_st, nth(b, 8, 0))
                sp.nop(nofuse=True)
                sp.dma_start(q_stack[0:64, :], qk_hl[0:64, :]).then_inc(b_stack, 16)
                sp.dma_start(k_stack[32:96, :], qk_hl[64:128, :]).then_inc(b_stack, 16)
                sp.dma_start(q_stack[64:96, :], qk_hl[0:32, :]).then_inc(b_stack, 16)
                sp.dma_start(k_stack[0:32, :], qk_hl[64:96, :]).then_inc(b_stack, 16)

            def a_regroup(b):
                sp.wait_ge(a_ol, nth(b, 2, 2))
                sp.nop(nofuse=True)
                after(sp, a_y, nth(b, 4, 0))
                sp.nop(nofuse=True)
                for r in range(4):
                    for s in range(4):
                        sp.dma_start(o_dst[32 * s:32 * s + 32, r], o_src[32 * r:32 * r + 32, s]).then_inc(a_ox, 16)

            def first(i, b, o, m, f):
                for j in range(3):
                    if o: store_pair(sp, i - 1, j)

            def second(i, b, o, m, f):
                if m: a_regroup(i + 1)
                if f and not (isinstance(i, int) and i + 3 >= IMAGES): load(i + 3)
                if m: b_stacks(i + 1)

            sp.dma_start(wp_f, w_proj.rearrange("(a p) n -> p a n", p=P)).then_inc(s_wp, 16)
            for n, w in enumerate((wq1, wq1, wk1, wk1)):
                sp.dma_start(wqk1_f[:, :, n * 32:(n + 1) * 32], w.rearrange("(a p) n -> p a n", p=P)).then_inc(s_wqk1, 16)
            load(0)
            second(-2, False, False, False, True)
            all_steps(sp, first, second)
            for j in range(4):
                sp.wait_ge(b_out[j], nth(IMAGES, 16, 0))

        @block.tensor
        def _(pe):
            def transposes(k, b, jobs):
                u = bufs[k]
                for j in jobs:
                    c, ct = divmod(j, CT)
                    if k == "a":
                        bank = j
                        pe.wait_ge(a_load[c], nth(b, 16, 16))
                        after(pe, a_sub, nth(b, 2, 0))
                    else:
                        bank = 2 + j % 2
                        pe.wait_ge(a_x1, nth(b, 4, 2 * (c + 1)))
                        if j < 2:
                            after(pe, b_vl, nth(b, 4, j - 1))
                        else:
                            pe.wait_ge(u["s_xt"], nth(b, 4, j - 1))
                    for t in range(TPC):
                        last = nc.tensor.transpose(u["ps"][:, bank, t * P:(t + 1) * P],
                                                   u["src"][:, c * TPC + t, ct * P:(ct + 1) * P], ident[:])
                    last.then_inc(u["s_tr"], 1)

            def group_mean(k, b):
                u = bufs[k]
                pe.wait_ge(u["s_mv"], nth(b, 2, 2))
                if k == "a":
                    after(pe, b_qkl, nth(b, 2, -2))
                nc.tensor.matmul(pb[:, 2, u["col"]:u["col"] + CT], group_avg[:], u["mv"][:, :, 0], start=True, stop=True).then_inc(u["s_gm"], 1)

            def group_var(k, b):
                u = bufs[k]
                pe.wait_ge(u["s_var"], nth(b, 1, 1))
                nc.tensor.matmul(pb[:, 3, u["col"]:u["col"] + CT], group_avg[:], u["e"][:], start=True, stop=True).then_inc(u["s_gv"], 1)

            def project_T(out_ap, wh, wl, cols, c, nh, nl):
                tok = slice(c * CHUNK, (c + 1) * CHUNK)
                for ct in range(CT):
                    last = split3(out_ap, (wh[:, ct, cols], wl[:, ct, cols]), (nh[:, ct, tok], nl[:, ct, tok]),
                                  start=(ct == 0), stop=(ct == CT - 1))
                return last

            def project(out_ap, lhs, wh, wl, cols):
                for ct in range(CT):
                    last = split3(out_ap, (lhs[0][:, ct], lhs[1][:, ct]), (wh[:, ct, cols], wl[:, ct, cols]),
                                  start=(ct == 0), stop=(ct == CT - 1))
                return last

            def a_project_qk(b, c, ds):
                for d in ds:
                    pe.wait_ge(n_["a"]["nl"], nth(b, 4, 2 * c + 2))
                    if c == 0:
                        after(pe, a_ol, nth(b, 2, 0))
                    elif d < 2:
                        pe.wait_ge(a_qe, nth(b, 4, d + 1))
                    elif isinstance(b, int) and b == 0:
                        pe.wait_ge(a_ke, nth(b, 4, d - 1))
                    else:
                        pe.wait_ge(a_x1, nth(b, 4, d - 3))
                    project_T(pa[:, d, :], wqkv_h, wqkv_l, slice(d * P, (d + 1) * P), c, a_nh, a_nl).then_inc(a_qk, 1)

            def a_project_v(b, js):
                for j in js:
                    if j < 2:
                        after(pe, b_eh, nth(b, 8, -8))
                    else:
                        pe.wait_ge(a_ve, nth(b, 4, j - 1))
                    for t in range(2):
                        tok = slice((2 * j + t) * P, (2 * j + t + 1) * P)
                        last = project(pb[:, j % 2, t * CH:(t + 1) * CH], (a_nh[:, :, tok], a_nl[:, :, tok]),
                                       wqkv_h, wqkv_l, slice(2 * CH, 3 * CH))
                    last.then_inc(a_v, 1)

            def a_scores(b, ts):
                if ts[0] == 0:
                    pe.wait_ge(a_qe, nth(b, 4, 4))
                    pe.wait_ge(a_ke, nth(b, 4, 4))
                    pe.nop(nofuse=True)
                if ts[0] == TPC:
                    pe.wait_ge(a_sub, nth(b, 2, 1))
                    pe.nop(nofuse=True)
                for t in ts:
                    for g in range(2):
                        for w in range(4):
                            n = t * 4 + w
                            tok = slice(n * WIN, (n + 1) * WIN)
                            for r in range(4):
                                rows = slice(32 * r, 32 * r + 32)
                                col = (2 * (t % TPC) + g) * WIN
                                last = nc.tensor.matmul(pa[32 * w:32 * w + 32, r, col:col + WIN],
                                                        qkT[rows, g, tok], qkT[rows, 2 + g, tok], start=True, stop=True)
                if ts[-1] % TPC == TPC - 1:
                    last.then_inc(a_s, 1)

            def a_output(b, b_next, ts):
                if ts[0] == 0:
                    pe.wait_ge(a_pt, nth(b, 2, 2))
                    pe.nop(nofuse=True)
                    if b_next:
                        pe.wait_ge(n_["a"]["xt"], nth(b, 4, 8))
                        pe.nop(nofuse=True)
                for t in ts:
                    for g in range(2):
                        for r in range(4):
                            h = 4 * g + r
                            blk = (r * 8 + 2 * (t % TPC) + g) * WIN
                            for w in range(4):
                                rows = slice(32 * w, 32 * w + 32)
                                col = (2 * t + g) * WIN
                                last = nc.tensor.matmul(pa[32 * r:32 * r + 32, w, col:col + WIN], v_tok[rows, t, h * DH:(h + 1) * DH],
                                                        pT[rows, t // TPC, blk:blk + WIN], start=True, stop=True)
                if ts[-1] == TILES - 1:
                    last.then_inc(a_o, 1)

            def a_projection(b, b_next, js):
                for j in js:
                    pe.wait_ge(a_ox, nth(b, 256, 256))
                    if j >= 2:
                        pe.wait_ge(a_x1, nth(b, 4, j - 1))
                    elif b_next:
                        pe.wait_ge(a_ke, nth(b, 4, j + 5))
                    for t in range(2):
                        h = 2 * j + t
                        lhs = [o_dst[:, h % 4, :, part, h // 4, :] for part in (0, 1)]
                        last = project(pa[:, 2 + j % 2, t * CH:(t + 1) * CH], lhs, wp_h, wp_l, slice(0, CH))
                    last.then_inc(a_y, 1)

            def b_project_qk(b, c):
                pe.wait_ge(n_["b"]["nl"], nth(b, 4, 2 * c + 2))
                project_T(pb[:, 2 + c, :], wqk1_h, wqk1_l, slice(0, P), c, b_nh, b_nl).then_inc(b_qk, 1)

            def b_project_v(b, f, js):
                for j in js:
                    if f and j == 0:
                        pe.wait_ge(n_["a"]["ve"], nth(b, 1, 3))
                    if j < 2:
                        after(pe, b_y, nth(b, 8, j - 1))
                    else:
                        pe.wait_ge(b_vl, nth(b, 4, j - 1))
                    for t in range(2):
                        tok = slice((2 * j + t) * P, (2 * j + t + 1) * P)
                        last = project(pb[:, 2 + j % 2, t * CH:(t + 1) * CH], (b_nh[:, :, tok], b_nl[:, :, tok]), wv1_h, wv1_l, slice(0, CH))
                    last.then_inc(b_v, 1)

            def b_energy(b, it, b_next):
                pe.wait_ge(b_stack, nth(b, 64, 64))
                if it == 0 and b_next:
                    pe.wait_ge(a_ve, nth(b, 4, 8))
                elif it == 0:
                    after(pe, b_eh, nth(b, 8, 0))
                else:
                    pe.wait_ge(b_max, nth(b, 8, it))
                for c in range(CHUNKS):
                    last = nc.tensor.matmul(pb[:, c, :], k_stack[0:96, it * P:(it + 1) * P],
                                            q_stack[0:96, c * CHUNK:(c + 1) * CHUNK], start=True, stop=True)
                last.then_inc(b_s, 1)

            def b_max_rows(b):
                pe.wait_ge(b_dup, nth(b, 1, 1))
                for it in range(TILES):
                    last = nc.tensor.matmul(pb[96:98, it // TPC, (it % TPC) * P:(it % TPC + 1) * P],
                                            max_dup[:, it, :], ident[:], start=True, stop=True)
                last.then_inc(b_row, 1)

            def b_energy_T(b, jt):
                if jt == 0:
                    pe.wait_ge(b_rowl, nth(b, 1, 1))
                else:
                    pe.wait_ge(b_eh, nth(b, 8, jt))
                for c in range(CHUNKS):
                    last = nc.tensor.matmul(pb[:, c, :], q_stack[0:98, jt * P:(jt + 1) * P],
                                            k_stack[0:98, c * CHUNK:(c + 1) * CHUNK], start=True, stop=True)
                last.then_inc(b_st, 1)

            def b_output(b, it, b_next, jts=range(TILES)):
                if last_image(b):
                    pe.wait_ge(b_el, nth(b, 8, jts[-1] + 1))
                    if it >= 6:
                        pe.wait_ge(b_y, nth(b, 8, it - 5))
                elif jts[0] == 0:
                    pe.wait_ge(b_el, nth(b, 8, 8))
                    if it >= 2:
                        pe.wait_ge(b_y, nth(b, 8, it - 1))
                    elif b_next:
                        pe.wait_ge(b_qkl, nth(b, 2, 3 + it))
                    else:
                        pe.wait_ge(b_vl, nth(b, 4, 4))
                rows = slice(it * P, (it + 1) * P)
                for jt in jts:
                    last = split3(result_bank(b, it)[:, 0:CH + 1], (e_h[:, jt, rows], e_l[:, jt, rows]),
                                  (v_h[:, jt, 0:CH + 1], v_l[:, jt, 0:CH + 1]), start=(jt == 0), stop=(jt == TILES - 1))
                if jts[-1] == TILES - 1:
                    last.then_inc(b_pv, 1)

            def first(i, b, o, m, f):
                for it in range(4):
                    if o and not last_image(i - 1): b_output(i - 1, it, b, range(0, 4))
                    if m and it < 2: a_scores(i + 1, (2 * it + 4,))
                    if b and it == 1: b_energy(i, 0, m)
                    if f and it == 3: transposes("a", i + 2, range(4))
                    if o and not last_image(i - 1): b_output(i - 1, it, b, range(4, 8))
                    if b and it >= 1: b_energy(i, it, m)
                    if m and it < 2: a_scores(i + 1, (2 * it + 5,))
                for it in range(4, 8):
                    if o and last_image(i - 1):
                        if it >= 6: b_output(i - 1, it, b)
                        continue
                    if o: b_output(i - 1, it, b, range(0, 4))
                    if m: a_output(i + 1, f, (2 * it - 8,))
                    if b and it == 7: b_energy(i, it, m)
                    if m and it == 7: a_output(i + 1, f, (7,))
                    if o: b_output(i - 1, it, b, range(4, 8))
                    if m and it < 7: a_output(i + 1, f, (2 * it - 7,))
                    if b and it < 7: b_energy(i, it, m)
                    if f and it == 4: group_mean("a", i + 2)
                    if f and it == 5: group_var("a", i + 2)

            def outputs_behind(b, jt):
                if jt == 0:
                    pe.wait_ge(b_vl, nth(b, 4, 4))
                for it in range(6):
                    b_output(b, it, False, (jt,))

            def second(i, b, o, m, f):
                if b: b_max_rows(i)
                if b: b_project_v(i, f, (0, 1))
                if b: b_energy_T(i, 0)
                if b: b_project_v(i, f, (2,))
                if f: a_project_qk(i + 2, 0, (0,))
                if b: b_energy_T(i, 1)
                if f: a_project_qk(i + 2, 0, (1,))
                if b: b_project_v(i, f, (3,))
                if b: b_energy_T(i, 2)
                if f: a_project_qk(i + 2, 0, (2, 3))
                if b: b_energy_T(i, 3)
                if last_image(i): outputs_behind(i, 0)
                if f: a_project_qk(i + 2, 1, (0, 1))
                if b: b_energy_T(i, 4)
                if last_image(i): outputs_behind(i, 1)
                if m: a_projection(i + 1, f, (0, 1))
                if b: b_energy_T(i, 5)
                if last_image(i): outputs_behind(i, 2)
                if m: a_projection(i + 1, f, (2,))
                if m: transposes("b", i + 1, (0, 1))
                if m: a_projection(i + 1, f, (3,))
                if b: b_energy_T(i, 6)
                if last_image(i): outputs_behind(i, 3)
                if f: a_project_qk(i + 2, 1, (2,))
                if m: transposes("b", i + 1, (2, 3))
                if b: b_energy_T(i, 7)
                for jt in range(4, 8):
                    if last_image(i): outputs_behind(i, jt)
                if f: a_project_qk(i + 2, 1, (3,))
                for j in range(4):
                    if f: a_scores(i + 2, (j,))
                    if f: a_project_v(i + 2, (j,))
                    if m and j == 0: group_mean("b", i + 1)
                    if m and j == 1: group_var("b", i + 1)
                for c in range(CHUNKS):
                    if m: b_project_qk(i + 1, c)

            pe.wait_ge(s_const, 80)
            pe.wait_ge(s_wmax, 1)
            nc.tensor.transpose(pb[0:5, 0, 0:P], wmax[:], ident[:]).then_inc(s_wmaxT, 1)
            pe.wait_ge(s_diag, 1)
            nc.tensor.matmul(pb[:, 1, 0:5], ones5[:], wmax_diag[:], start=True, stop=True).then_inc(s_unit_ps, 1)
            first(-2, False, False, False, True)
            pe.wait_ge(s_ready, 1)
            second(-2, False, False, False, True)
            pe.wait_ge(s_ready, 5)
            pe.wait_ge(s_pool, 5)
            all_steps(pe, first, second)

        @block.scalar
        def _(act):
            def copy_T(k, b, jobs):
                u = bufs[k]
                for j in jobs:
                    c, ct = divmod(j, CT)
                    act.wait_ge(u["s_tr"], nth(b, 4, j + 1))
                    nc.scalar.activation(u["xT"][:, ct, c * CHUNK:(c + 1) * CHUNK], u["ps"][:, j if k == "a" else 2 + j % 2, :], ACT.Copy).then_inc(u["s_xt"], 1)

            def normalise(k, b, last):
                u = bufs[k]
                act.wait_ge(u["s_nb"], nth(b, 1, 1))
                for c in range(CHUNKS):
                    for ct in range(CT):
                        j = c * CT + ct
                        if last is not None:
                            act.wait_ge(n_[last[0]]["nl"], nth(last[1], 4, j + 1))
                        if k == "a":
                            src = u["xT"][:, ct, :].rearrange("p (w t k) -> p t w k", w=4, k=WIN)[:, c * TPC:(c + 1) * TPC]
                            dst = u["xn"][:, j, :].rearrange("p (t w k) -> p t w k", w=4, k=WIN)
                        else:
                            src, dst = u["xT"][:, ct, c * CHUNK:(c + 1) * CHUNK], u["xn"][:, j, :]
                        nc.scalar.activation(dst, src, ACT.Identity,
                                             scale=u["r"][:, ct:ct + 1], bias=u["nb"][:, ct:ct + 1]).then_inc(u["s_xn"], 1)

            def a_copy_q(b, c):
                for d in range(2):
                    act.wait_ge(a_qk, nth(b, 8, 4 * c + d + 1))
                    after(act, a_s, nth(b, 2, 0))
                    for u in range(2):
                        last = nc.scalar.activation(
                            qkT[:, d, c * CHUNK:(c + 1) * CHUNK].rearrange("p (n s u i) -> p u n s i", s=4, u=2, i=4)[:, u],
                            pa[:, d, :].rearrange("p (n i u s) -> p u n s i", s=4, u=2, i=4)[:, u], ACT.Copy, scale=f_q[:, 0:1])
                    last.then_inc(a_qe, 1)

            def a_copy_v(b, js):
                for j in js:
                    act.wait_ge(a_v, nth(b, 4, j + 1))
                    after(act, a_o, nth(b, 1, 0))
                    nc.scalar.activation(v_tok[:, 2 * j:2 * j + 2, :].rearrange("p t n -> p (t n)"), pb[:, j % 2, :], ACT.Copy).then_inc(a_ve, 1)

            def a_exponential(b, c):
                act.wait_ge(a_sub, nth(b, 2, c + 1))
                nc.scalar.activation(s32[:, c, :], s32[:, c, :], ACT.Exp).then_inc(a_exp, 1)

            def a_out_high(b):
                act.wait_ge(a_o, nth(b, 1, 1))
                after(act, a_ox, nth(b, 256, 0))
                for g in range(2):
                    last = nc.scalar.activation(out_parts(0, g), out_banks(g), ACT.Copy)
                last.then_inc(a_oh, 1)

            def b_qk_high(b):
                for c in range(CHUNKS):
                    act.wait_ge(b_qk, nth(b, 2, c + 1))
                    nc.scalar.activation(qk_h[:, c * CHUNK:(c + 1) * CHUNK], pb[:, 2 + c, :], ACT.Copy).then_inc(b_qkh, 1)

            def b_v_high(b, js):
                for j in js:
                    act.wait_ge(b_v, nth(b, 4, j + 1))
                    after(act, b_pv, nth(b, 8, 0))
                    nc.scalar.activation(v_h[:, 2 * j:2 * j + 2, 0:CH], pb[:, 2 + j % 2, :].rearrange("p (t n) -> p t n", t=2), ACT.Copy).then_inc(b_vh, 1)

            def b_row_high(b):
                act.wait_ge(b_row, nth(b, 1, 1))
                nc.scalar.activation(max_row[96:98, :], pb[96:98, 0:2, :].rearrange("p a n -> p (a n)"), ACT.Copy).then_inc(b_rowh, 1)

            def b_exponential(b, jt):
                act.wait_ge(b_st, nth(b, 8, jt + 1))
                after(act, b_el, nth(b, 8, jt - 1))
                src = pb[:, 0:2, :].rearrange("p a n -> p (a n)")
                nc.scalar.activation(e32[:, jt % 2, :], src, ACT.Exp, scale=f_energy[:, 0:1]).then_inc(b_exp, 1)
                nc.scalar.activation(e_h[:, jt, :], src, ACT.Exp, scale=f_energy[:, 0:1]).then_inc(b_eh, 1)

            def first(i, b, o, m, f):
                if m: a_exponential(i + 1, 1)
                if f: copy_T("a", i + 2, range(4))
                if f: normalise("a", i + 2, ("b", i) if b else ("a", i + 1) if m else None)
                if m: a_out_high(i + 1)

            def second(i, b, o, m, f):
                if b: b_row_high(i)
                if b: b_v_high(i, (0, 1))
                if b: b_exponential(i, 0)
                if o: store_pair(act, i - 1, 3)
                if b: b_exponential(i, 1)
                if b: b_v_high(i, (2,))
                if f: a_copy_q(i + 2, 0)
                if b: b_v_high(i, (3,))
                if b: b_exponential(i, 2)
                if b: b_exponential(i, 3)
                if f: a_copy_q(i + 2, 1)
                for jt in range(4, 6):
                    if b: b_exponential(i, jt)
                if m: copy_T("b", i + 1, (0, 1))
                if b: b_exponential(i, 6)
                if m: copy_T("b", i + 1, (2, 3))
                if b: b_exponential(i, 7)
                if f: a_copy_v(i + 2, (0, 1))
                if m: normalise("b", i + 1, ("a", i + 2) if f else ("b", i))
                if f: a_copy_v(i + 2, (2, 3))
                if m: b_qk_high(i + 1)
                if f: a_exponential(i + 2, 0)

            act.dma_start(wqkv_f, w_qkv.rearrange("(a p) n -> p a n", p=P)).then_inc(s_wqkv, 16)
            act.dma_start(wv1_f, wv1.rearrange("(a p) n -> p a n", p=P)).then_inc(s_wv1, 16)
            act.dma_start(group_avg[:], group_d).then_inc(s_const, 16)
            act.dma_start(masks[:], masks_d).then_inc(s_const, 16)
            act.dma_start(bias[:], b_proj.rearrange("(o n) -> o n", o=1).broadcast_to([P, CH])).then_inc(s_const, 16)
            act.dma_start(gam[:], gamma.rearrange("(o n) -> o n", o=1).broadcast_to([P, 1])).then_inc(s_const, 16)

            def weights_high(ns):
                for n in ns:
                    w, h, l, u = scaled[n]
                    nc.scalar.activation(h, w, ACT.Copy, scale=unit_inv[:, u:u + 1]).then_inc(s_high, 1)

            act.wait_ge(s_unit, 1)
            weights_high((0,))
            first(-2, False, False, False, True)
            weights_high(range(1, 5))
            second(-2, False, False, False, True)
            all_steps(act, first, second)

        @block.vector
        def _(dve):
            def stats(k, b):
                u = bufs[k]
                for c in range(CHUNKS):
                    for ct in range(CT):
                        dve.wait_ge(u["s_xt"], nth(b, 4, c * CT + ct + 1))
                        nc.vector.bn_stats(u["st"][:, ct, c, :], u["xT"][:, ct, c * CHUNK:(c + 1) * CHUNK]).then_inc(u["s_bn"], 1)
                dve.wait_ge(u["s_bn"], nth(b, 4, 4))
                dve.nop(nofuse=True)
                for ct in range(CT):
                    nc.vector.bn_aggr(u["mv"][:, ct, :], u["st"][:, ct].rearrange("p c s -> p (c s)")).then_inc(u["s_mv"], 1)

            def group_mean(k, b):
                u = bufs[k]
                dve.wait_ge(u["s_gm"], nth(b, 1, 1))
                nc.vector.tensor_scalar(u["gm"][:], pb[:, 2, u["col"]:u["col"] + CT], -1.0, None, ALU.mult).then_inc(u["s_gmc"], 1)
                dve.wait_ge(u["s_gmc"], nth(b, 1, 1))
                nc.vector.tensor_tensor(u["d"][:], u["mv"][:, :, 0], u["gm"][:], ALU.add).then_inc(u["s_dev"], 1)
                dve.wait_ge(u["s_dev"], nth(b, 1, 1))
                nc.vector.tensor_tensor(u["e"][:], u["d"][:], u["d"][:], ALU.mult).then_inc(u["s_sq"], 1)
                dve.wait_ge(u["s_sq"], nth(b, 1, 1))
                nc.vector.tensor_tensor(u["e"][:], u["e"][:], u["mv"][:, :, 1], ALU.add).then_inc(u["s_var"], 1)

            def group_scale(k, b):
                u = bufs[k]
                dve.wait_ge(u["s_gv"], nth(b, 1, 1))
                nc.vector.tensor_scalar(u["ve"][:], pb[:, 3, u["col"]:u["col"] + CT], EPS, None, ALU.add).then_inc(u["s_ve"], 1)

            def norm_high(k, b):
                u = bufs[k]
                for c in range(CHUNKS):
                    for ct in range(CT):
                        j = c * CT + ct
                        dve.wait_ge(u["s_xn"], nth(b, 4, j + 1))
                        after(dve, a_v if k == "a" else b_v, nth(b, 4, 0))
                        nc.vector.tensor_copy(u["nh"][:, ct, c * CHUNK:(c + 1) * CHUNK], u["xn"][:, j, :]).then_inc(u["s_nh"], 1)

            def a_copy_k(b, c):
                for d in range(2, 4):
                    dve.wait_ge(a_qk, nth(b, 8, 4 * c + d + 1))
                    after(dve, a_s, nth(b, 2, 0))
                    nc.vector.tensor_copy(qkT[:, d, c * CHUNK:(c + 1) * CHUNK], pa[:, d, :]).then_inc(a_ke, 1)

            heads4 = dict(n=8, k=WIN)

            def a_maximum(b, c):
                dve.wait_ge(a_s, nth(b, 2, c + 1))
                s = pa[:, :, 0:CH].rearrange("p r (n k) -> p r n k", **heads4)
                m = a_rmax[:, c, :].rearrange("p (r n) -> p r n", r=4)
                nc.vector.tensor_reduce(m, s, X, ALU.max).then_inc(a_max, 1)
                dve.wait_ge(a_max, nth(b, 2, c + 1))
                nc.vector.tensor_tensor(s32[:, c, :].rearrange("p (r n k) -> p r n k", r=4, k=WIN), s,
                                        m.unsqueeze(3).broadcast_to([P, 4, 8, WIN]), ALU.subtract).then_inc(a_sub, 1)

            def a_row_sum(b, c):
                dve.wait_ge(a_exp, nth(b, 2, c + 1))
                nc.vector.tensor_reduce(a_rsum[:, c, :], s32[:, c, :].rearrange("p (n k) -> p n k", k=WIN), X, ALU.add).then_inc(a_sum, 1)
                dve.wait_ge(a_sum, nth(b, 2, c + 1))
                nc.vector.reciprocal(a_rinv[:, c, :], a_rsum[:, c, :]).then_inc(a_inv, 1)

            def a_transpose(b, c):
                dve.wait_ge(a_prob, nth(b, 2, c + 1))
                after(dve, a_o, nth(b, 1, 0))
                nc.vector.transpose(pT[:, c, :], s32[:, c, :]).then_inc(a_pt, 1)

            def a_out_low(b, g):
                dve.wait_ge(a_oh, nth(b, 1, 1))
                nc.vector.tensor_tensor(out_parts(1, g), out_banks(g), out_parts(0, g), ALU.subtract).then_inc(a_ol, 1)

            def a_residual(b, js):
                dve.wait_ge(a_xb, nth(b, 1, 1))
                after(dve, n_["b"]["tr"], nth(b, 4, 0))
                for j in js:
                    after(dve, b_copy, nth(b, 4, j - 3))
                    dve.wait_ge(a_y, nth(b, 4, j + 1))
                    nc.vector.scalar_tensor_tensor(x1[:, 2 * j:2 * j + 2, :].rearrange("p t n -> p (t n)"), pa[:, 2 + j % 2, :], f_proj[:, 0:1],
                                                   xb[:, 2 * j:2 * j + 2, :].rearrange("p t n -> p (t n)"), ALU.mult, ALU.add).then_inc(a_x1, 1)

            def b_qk_low(b):
                after(dve, b_stack, nth(b, 64, 0))
                for c in range(CHUNKS):
                    dve.wait_ge(b_qkh, nth(b, 2, c + 1))
                    cols = slice(c * CHUNK, (c + 1) * CHUNK)
                    nc.vector.scalar_tensor_tensor(qk_hl[:, cols], qk_h[:, cols], masks[:, 0:1], pb[:, 2 + c, :],
                                                   ALU.mult, ALU.add).then_inc(b_qkl, 1)

            def b_v_low(b, js):
                for j in js:
                    dve.wait_ge(b_vh, nth(b, 4, j + 1))
                    nc.vector.tensor_tensor(v_l[:, 2 * j:2 * j + 2, 0:CH], pb[:, 2 + j % 2, :].rearrange("p (t n) -> p t n", t=2),
                                            v_h[:, 2 * j:2 * j + 2, 0:CH], ALU.subtract).then_inc(b_vl, 1)

            def b_maximum(b, it):
                dve.wait_ge(b_s, nth(b, 8, it + 1))
                nc.vector.tensor_reduce(max_neg[:, it:it + 1], pb[:, 0:2, :].rearrange("p a n -> p (a n)"),
                                        X, ALU.max, negate=True).then_inc(b_max, 1)

            def b_duplicate(b):
                dve.wait_ge(b_max, nth(b, 8, 8))
                nc.vector.tensor_scalar(max_dup[:], max_neg[:].unsqueeze(2).broadcast_to([P, TILES, 2]),
                                        1.0 / ROW_SCALE, None, ALU.mult).then_inc(b_dup, 1)

            def b_row_low(b):
                dve.wait_ge(b_rowh, nth(b, 1, 1))
                nc.vector.scalar_tensor_tensor(k_stack[96:98, :], max_row[96:98, :], masks[96:98, 1:2],
                                               pb[96:98, 0:2, :].rearrange("p a n -> p (a n)"), ALU.mult, ALU.add).then_inc(b_rowl, 1)

            def b_exp_low(b, jt):
                dve.wait_ge(b_eh, nth(b, 8, jt + 1))
                nc.vector.tensor_tensor(e_l[:, jt, :], e32[:, jt % 2, :], e_h[:, jt, :], ALU.subtract).then_inc(b_el, 1)

            def b_result(b, it):
                dve.wait_ge(b_copy, nth(b, 4, it // 2 + 1))
                dve.wait_ge(b_pv, nth(b, 8, it + 1))
                nc.vector.reciprocal(y_inv[:, it:it + 1], result_bank(b, it)[:, CH:CH + 1]).then_inc(b_yinv, 1)
                dve.wait_ge(b_yinv, nth(b, 8, it + 1))
                nc.vector.tensor_tensor(y_fac[:, it:it + 1], y_inv[:, it:it + 1], f_out[:, 0:1], ALU.mult).then_inc(b_yfac, 1)
                dve.wait_ge(b_yfac, nth(b, 8, it + 1))
                nc.vector.scalar_tensor_tensor(y[:, it, :], result_bank(b, it)[:, 0:CH], y_fac[:, it:it + 1], y[:, it, :],
                                               ALU.mult, ALU.add).then_inc(b_y, 1)

            def first(i, b, o, m, f):
                if m: a_row_sum(i + 1, 0)
                if o: b_result(i - 1, 0)
                if m: a_transpose(i + 1, 0)
                if b: b_maximum(i, 0)
                if b: b_maximum(i, 1)
                if m: a_maximum(i + 1, 1)
                if o: b_result(i - 1, 1)
                if m: a_row_sum(i + 1, 1)
                if b: b_maximum(i, 2)
                if o: b_result(i - 1, 2)
                if m: a_transpose(i + 1, 1)
                if b: b_maximum(i, 3)
                if f: stats("a", i + 2)
                if o: b_result(i - 1, 3)
                if b: b_maximum(i, 4)
                if f: group_mean("a", i + 2)
                if o: b_result(i - 1, 4)
                if b: b_maximum(i, 5)
                if f: group_scale("a", i + 2)
                if o: b_result(i - 1, 5)
                if b: b_maximum(i, 6)
                if f: norm_high("a", i + 2)
                if o: b_result(i - 1, 6)
                if b: b_maximum(i, 7)
                if b: b_duplicate(i)
                if o: b_result(i - 1, 7)

            def second(i, b, o, m, f):
                if m: a_out_low(i + 1, 0)
                if b: b_row_low(i)
                if b: b_v_low(i, (0,))
                if m: a_out_low(i + 1, 1)
                if b: b_v_low(i, (1,))
                if b: b_exp_low(i, 0)
                if b: b_v_low(i, (2, 3))
                if b: b_exp_low(i, 1)
                if f: a_copy_k(i + 2, 0)
                if b: b_exp_low(i, 2)
                if b: b_exp_low(i, 3)
                if m: a_residual(i + 1, (0,))
                if b: b_exp_low(i, 4)
                if m: a_residual(i + 1, (1,))
                if b: b_exp_low(i, 5)
                if m: a_residual(i + 1, (2, 3))
                if b: b_exp_low(i, 6)
                if f: a_copy_k(i + 2, 1)
                if m: stats("b", i + 1)
                if m: group_mean("b", i + 1)
                if b: b_exp_low(i, 7)
                if m: group_scale("b", i + 1)
                if m: norm_high("b", i + 1)
                if f: a_maximum(i + 2, 0)
                if m: b_qk_low(i + 1)

            chain = [0]

            def link(ins):
                chain[0] += 1
                ins.then_inc(s_chain, 1)
                dve.wait_ge(s_chain, chain[0])

            for n, w, landed, count in ((0, wqkv_f, s_wqkv, 16), (1, wp_f, s_wp, 16), (2, wqk1_f[:, :, 0:32], s_wqk1, 64),
                                        (3, wqk1_f[:, :, 64:96], s_wqk1, 64), (4, wv1_f, s_wv1, 16)):
                dve.wait_ge(landed, count)
                last = nc.vector.tensor_reduce(wmax[:, n:n + 1], w, mybir.AxisListType.XY, ALU.max, apply_absolute_value=True)
            last.then_inc(s_wmax, 1)
            dve.wait_ge(s_const, 80)
            dve.wait_ge(s_wmaxT, 1)
            link(nc.vector.tensor_reduce(wmax_all[:], pb[0:5, 0, 0:P], X, ALU.max))
            link(nc.vector.tensor_scalar(wmax_all[:], wmax_all[:], 1e-30, 2.0, ALU.max, ALU.mult))
            link(nc.vector.memset(ones5[:], 1.0))
            nc.vector.tensor_scalar(wmax_diag[:], ident[0:5, 0:5], wmax_all[:, 0:1], None, ALU.mult).then_inc(s_diag, 1)
            dve.wait_ge(s_unit_ps, 1)
            link(nc.vector.tensor_copy(unit[:], pb[:, 1, 0:5]))
            nc.vector.reciprocal(unit_inv[:], unit[:]).then_inc(s_unit, 1)
            link(nc.vector.scalar_tensor_tensor(f_q[:], unit[:, 0:1], DH ** -0.5, unit[:, 0:1], ALU.mult, ALU.mult))
            link(nc.vector.tensor_tensor(f_proj[:], unit[:, 0:1], unit[:, 1:2], ALU.mult))
            link(nc.vector.tensor_tensor(f_energy[:], unit[:, 2:3], unit[:, 3:4], ALU.mult))
            link(nc.vector.tensor_tensor(f_out[:], unit[:, 4:5], gam[:], ALU.mult))
            def weights_low(ns):
                for n in ns:
                    w, h, l, u = scaled[n]
                    dve.wait_ge(s_high, n + 1)
                    nc.vector.scalar_tensor_tensor(l, w, unit_inv[:, u:u + 1], h, ALU.mult, ALU.subtract).then_inc(s_ready, 1)

            weights_low((0,))
            first(-2, False, False, False, True)
            weights_low(range(1, 5))
            second(-2, False, False, False, True)
            all_steps(dve, first, second)

        @block.gpsimd
        def _(pool):
            def rstd(k, b):
                u = bufs[k]
                pool.wait_ge(u["s_ve"], nth(b, 1, 1))
                nc.gpsimd.tensor_tensor(u["r"][:], u["ve"][:], minus_half[:], ALU.pow).then_inc(u["s_r"], 1)
                pool.wait_ge(u["s_r"], nth(b, 1, 1))
                nc.gpsimd.tensor_tensor(u["nb"][:], u["gm"][:], u["r"][:], ALU.mult).then_inc(u["s_nb"], 1)

            def norm_low(k, b):
                u = bufs[k]
                for c in range(CHUNKS):
                    for ct in range(CT):
                        j = c * CT + ct
                        cols = slice(c * CHUNK, (c + 1) * CHUNK)
                        pool.wait_ge(u["s_nh"], nth(b, 4, j + 1))
                        nc.gpsimd.tensor_tensor(u["nl"][:, ct, cols], u["xn"][:, j, :], u["nh"][:, ct, cols], ALU.subtract).then_inc(u["s_nl"], 1)

            def add_bias(b):
                for c in range(CHUNKS):
                    pool.wait_ge(a_load[c], nth(b, 16, 16))
                after(pool, a_x1, nth(b, 4, 0))
                nc.gpsimd.tensor_tensor(xb[:], xin[:], bias[:].unsqueeze(1).broadcast_to([P, TILES, CH]), ALU.add).then_inc(a_xb, 1)

            def a_probabilities(b, c):
                pool.wait_ge(a_inv, nth(b, 2, c + 1))
                v = s32[:, c, :].rearrange("p (n k) -> p n k", k=WIN)
                nc.gpsimd.tensor_tensor(v, v, a_rinv[:, c, :].unsqueeze(2).broadcast_to([P, 32, WIN]), ALU.mult).then_inc(a_prob, 1)

            def b_keep(b, j):
                pool.wait_ge(a_x1, nth(b, 4, j + 1))
                after(pool, b_out[j], nth(b, 16, 0))
                pool.nop(nofuse=True)
                nc.gpsimd.tensor_copy(y[:, 2 * j:2 * j + 2, :], x1[:, 2 * j:2 * j + 2, :]).then_inc(b_copy, 1)

            def first(i, b, o, m, f):
                if m: a_probabilities(i + 1, 0)
                if m: a_probabilities(i + 1, 1)
                if b: b_keep(i, 0)
                if f: rstd("a", i + 2)
                if f: norm_low("a", i + 2)
                for j in (1, 2):
                    if b: b_keep(i, j)

            def second(i, b, o, m, f):
                if b: b_keep(i, 3)
                if f: add_bias(i + 2)
                if m: rstd("b", i + 1)
                if m: norm_low("b", i + 1)

            nc.gpsimd.memset(q_stack[96:128, :], ROW_SCALE).then_inc(s_pool, 1)
            pool.wait_ge(s_pool, 1)
            nc.gpsimd.memset(k_stack[96:128, :], 0.0).then_inc(s_pool, 1)
            pool.wait_ge(s_pool, 2)
            nc.gpsimd.memset(v_h[:, :, CH:VCOL], 1.0).then_inc(s_pool, 1)
            nc.gpsimd.memset(v_l[:, :, CH:VCOL], 0.0).then_inc(s_pool, 1)
            nc.gpsimd.memset(minus_half[:], -0.5).then_inc(s_pool, 1)
            pool.wait_ge(s_pool, 5)
            pool.wait_ge(s_const, 80)
            first(-2, False, False, False, True)
            second(-2, False, False, False, True)
            all_steps(pool, first, second)


_INS = ["x", "L0_conv_w_qkv", "L0_conv_w_proj", "L0_conv_b_proj", "L1_conv_Wq", "L1_conv_Wk", "L1_conv_Wv", "L1_conv_gamma"]


def kernel(**inputs):
    import numpy as _np
    import concourse.bacc as _bacc
    from concourse import mybir as _mybir
    from concourse.bass_utils import run_bass_kernel_spmd as _run

    nc = _bacc.Bacc("TRN2", target_bir_lowering=False, num_devices=1)
    arrays = {f"in_{name}": _np.ascontiguousarray(inputs[name]) for name in _INS}
    n = _np.arange(P)
    arrays["in_ident"] = _np.eye(P, dtype=_np.float32)
    arrays["in_group"] = _np.kron(_np.eye(P // GROUP), _np.full((GROUP, GROUP), 1.0 / GROUP)).astype(_np.float32)
    masks = _np.zeros((P, 2), _np.float32)
    masks[32:64, 0] = masks[96:128, 0] = -1.0
    masks[97, 1] = -1.0
    arrays["in_masks"] = masks
    args = [nc.dram_tensor(name, a.shape, _mybir.dt.from_np(a.dtype), kind="ExternalInput").ap() for name, a in arrays.items()]
    out = nc.dram_tensor("out_0", (IMAGES, 32, 32, CH), _mybir.dt.float32, kind="ExternalOutput").ap()
    build(nc, *args, out)
    r = _run(nc, [arrays], core_ids=[0])
    return r.results[0]["out_0"]
```
